# Optimizing a Trainium2 kernel written in Bass

```python
import numpy as np
import jax
import jax.numpy as jnp

def _softmax(x, axis=-1):
    return jax.nn.softmax(x, axis=axis)

def _gelu(x):
    return jax.nn.gelu(x, approximate=True)

def _silu(x):
    return jax.nn.silu(x)

def _sigmoid(x):
    return jax.nn.sigmoid(x)

def _layernorm(x, axis=-1, eps=1e-05):
    m = jnp.mean(x, axis=axis, keepdims=True)
    v = jnp.var(x, axis=axis, keepdims=True)
    return (x - m) / jnp.sqrt(v + eps)

def _scatter_add(tgt, idx, src, axis=0):
    return tgt.at[idx].add(src)

def _segment_sum(src, seg, n):
    return jax.ops.segment_sum(src, seg, n)
kernel_name = 'mk_gnn_preln_d1_gnn_r8_7be8d4'

def setup_inputs(seed: int=0):
    np.random.seed(seed)
    _w = jnp.asarray

    def _rec_inputs():
        import jax
        import jax.numpy as jnp
        _gk = jax.random.key(seed)
        x = -0.0006008 + 1.001 * jax.random.normal(jax.random.fold_in(_gk, 1), (6250, 256), jnp.float32)
        _s = jax.random.randint(jax.random.fold_in(_gk, 2), (100000,), 0, 6250, jnp.int32)
        _d = jax.random.randint(jax.random.fold_in(_gk, 3), (100000,), 0, 6250, jnp.int32)
        _loop = jnp.arange(6250, dtype=jnp.int32)
        src = jnp.concatenate([_s, _d, _loop])
        dst = jnp.concatenate([_d, _s, _loop])
        _o = jnp.argsort(dst, stable=True)
        src = src[_o]
        dst = dst[_o]
        edge_attr_64 = 0.000151818 + 1.00006 * jax.random.normal(jax.random.fold_in(_gk, 12), (206250, 64), jnp.float32)
        return (x, src, dst, edge_attr_64)
    x, src, dst, edge_attr_64 = _rec_inputs()

    def _L0_gnn_setup():
        import jax, jax.numpy as jnp
        import numpy as np
        N_NODES = 1250
        N_EDGES = 40000
        HIDDEN = 256
        N_RBF = 64
        key = jax.random.key(seed)
        k = jax.random.split(key, 8)
        h = jax.random.normal(k[0], (N_NODES, HIDDEN), dtype=jnp.float32)
        i = jax.random.randint(k[1], (N_EDGES,), 0, N_NODES)
        j = jax.random.randint(k[2], (N_EDGES,), 0, N_NODES)
        rbf = jax.random.normal(k[3], (N_EDGES, N_RBF), dtype=jnp.float32)
        s1 = 1.0 / np.sqrt(HIDDEN + N_RBF)
        s2 = 1.0 / np.sqrt(HIDDEN)
        W1 = jax.random.uniform(k[4], (HIDDEN + N_RBF, HIDDEN), minval=-s1, maxval=s1, dtype=jnp.float32)
        b1 = jax.random.uniform(k[5], (HIDDEN,), minval=-s1, maxval=s1, dtype=jnp.float32)
        W2 = jax.random.uniform(k[6], (HIDDEN, HIDDEN), minval=-s2, maxval=s2, dtype=jnp.float32)
        b2 = jax.random.uniform(k[7], (HIDDEN,), minval=-s2, maxval=s2, dtype=jnp.float32)
        return {'h': h, 'i': i, 'j': j, 'rbf': rbf, 'W1': W1, 'b1': b1, 'W2': W2, 'b2': b2}
    _L0_gnn_all = _L0_gnn_setup()
    _L0_gnn_in = {k: v for k, v in _L0_gnn_all.items() if k in ('W1', 'b1', 'W2', 'b2')}
    del _L0_gnn_all
    return {'x': x, 'src': src, 'dst': dst, 'edge_attr_64': edge_attr_64, 'L0_gnn_W1': _L0_gnn_in['W1'], 'L0_gnn_b1': _L0_gnn_in['b1'], 'L0_gnn_W2': _L0_gnn_in['W2'], 'L0_gnn_b2': _L0_gnn_in['b2']}

def reference(x, src, dst, edge_attr_64, L0_gnn_W1, L0_gnn_b1, L0_gnn_W2, L0_gnn_b2):
    import jax
    import jax.numpy as jnp

    def _L0_gnn_ref(h, i, j, rbf, W1, b1, W2, b2):
        import jax, jax.numpy as jnp
        import numpy as np
        N_NODES = 1250
        N_EDGES = 40000
        HIDDEN = 256
        N_RBF = 64
        m = jnp.concatenate([h[j], rbf], axis=-1)
        m = jax.nn.silu(m @ W1 + b1)
        m = m @ W2 + b2
        agg = jax.ops.segment_sum(m, i, num_segments=h.shape[0])
        return h + agg
    h = jnp.maximum(_layernorm(x, axis=-1), 0.0)
    x = x + _L0_gnn_ref(h, src, dst, edge_attr_64, L0_gnn_W1, L0_gnn_b1, L0_gnn_W2, L0_gnn_b2)
    return x

_drawn_inputs = setup_inputs


def setup_inputs(seed=0):
    import zlib

    import numpy as np

    out = dict(_drawn_inputs(seed))
    spreads = {}
    factors = {}
    for name, (base, spread) in spreads.items():
        noise = np.random.default_rng([zlib.crc32(name.encode()), seed]).standard_normal(out[name].shape)
        drawn = base * np.exp(spread * noise) if base else spread * noise
        out[name] = jnp.asarray(drawn.astype(out[name].dtype))
    for name, factor in factors.items():
        out[name] = (out[name] * factor).astype(out[name].dtype)
    return out
```

```python
import concourse.bass as bass
from concourse import mybir
from contextlib import ExitStack

P = 128


def gnn_layer_kernel(nc, x, src, dst, rbf, w1, b1, w2, b2, out):
    F32, I32 = mybir.dt.float32, mybir.dt.int32
    ALU, ACT, AX = mybir.AluOpType, mybir.ActivationFunctionType, mybir.AxisListType
    ds = bass.ds

    N, C = x.shape
    E, R = rbf.shape
    KC = C // P
    NB = -(-N // P)
    NF = N // P
    NR = N - NF * P
    CB = 7
    EPS = 1e-5

    G = 8
    H = G // 2
    GE = G * P
    GROUPS = E // GE
    TT = -(-(E - GROUPS * GE) // P)
    TBASE = E - TT * P
    OLD = GROUPS * GE - TBASE
    assert NR > 0 and NB % CB == 0 and TT == H and GROUPS % 2 == 1 and GROUPS >= 5
    K = 4
    W = C + 4
    Q = 8
    QB = P // Q
    V = W + Q
    NT = (NB + 1) * P
    ZR = NT // P // 2

    def scratch(name, shape):
        return nc.dram_tensor(name, shape, F32).ap()

    p_dram = scratch("p_rows", (N, C))
    tables = [scratch(f"table{k}", (NT, W)) for k in range(K)]

    rbf_groups = rbf[0:GROUPS * GE, :].rearrange("(g p j) r -> g p (j r)", p=P, j=G)
    src_groups = src[0:GROUPS * GE].rearrange("(g p j) -> g p j", p=P, j=G)
    dst_groups = dst[0:GROUPS * GE].rearrange("(g p j) -> g p j", p=P, j=G)
    rbf_tail = rbf[TBASE:E, :].rearrange("(p j) r -> p (j r)", p=P)
    src_tail = src[TBASE:E].rearrange("(p j) -> p j", p=P)
    dst_tail = dst[TBASE:E].rearrange("(p j) -> p j", p=P)

    ctx = ExitStack()
    with ctx:
        def sb(name, shape, dt=F32):
            return ctx.enter_context(nc.sbuf_tensor(name, shape, dt))

        def ps(name, shape):
            return ctx.enter_context(nc.psum_tensor(name, shape, F32))

        def sem(name):
            return ctx.enter_context(nc.semaphore(name))

        ident = sb("ident", [P, P])
        w1a = sb("w1a", [P, KC, C])
        w1b = sb("w1b", [P, C])
        w2s = sb("w2s", [P, KC, C])
        b1b = sb("b1b", [P, C])
        b2b = sb("b2b", [P, C])
        zero = sb("zero", [P, ZR * W])
        bits = sb("bits", [P, Q])
        below = sb("below", [P, Q], I32)
        belowf = sb("belowf", [P, Q])
        spare = sb("spare", [P, 1])
        fresh = sb("fresh", [P, H])
        stale = sb("stale", [P, H])
        xh = sb("xh", [P, NB, C])
        stats = sb("stats", [P, NB, 6])
        mom = sb("mom", [P, 4, NB])
        rstd = sb("rstd", [P, NB])
        nmr = sb("nmr", [P, NB])
        hs = sb("hs", [P, 2, C])
        hT = sb("hT", [P, 2, KC, P])
        prow = sb("prow", [P, 2, C])
        rbfs = sb("rbfs", [P, 2, G * R])
        srcs = sb("srcs", [P, 2, G], I32)
        dsts = sb("dsts", [P, 2, G], I32)
        srcf = sb("srcf", [P, 2, G])
        rbfT = sb("rbfT", [P, 2, H * P])
        pg = sb("pg", [P, 2, G, C])
        zs = sb("zs", [P, 2, H, C])
        act_rows = sb("act_rows", [P, 2, G, V])
        same = sb("same", [P, 2, H, P])
        sums = sb("sums", [P, 2, G, V])
        words = sb("words", [P, G, Q], I32)
        ahead = sb("ahead", [P, G, Q], I32)
        anyahead = sb("anyahead", [P, G])
        leads = sb("leads", [P, G])
        shifted = sb("shifted", [P, G])
        rows = sb("rows", [P, 2, G], I32)
        tabs = sb("tabs", [P, 2, K, W])
        pair = sb("pair", [P, 2, K // 2, W])
        cnt = sb("cnt", [P, 2, 1])
        sT = sb("sT", [P, 2, KC, P])
        base = sb("base", [P, 2, C])
        outs = sb("outs", [P, 2, C])

        ps_t = ps("ps_t", [P, H, P])
        ps_b = ps("ps_b", [P, H, P])
        ps_z = ps("ps_z", [P, 2, 2, 512])
        ps_s = ps("ps_s", [P, 2, 512])

        consts_in, consts_done = sem("consts_in"), sem("consts_done")
        pool_step, pool_turn, sp_turn = sem("pool_step"), sem("pool_turn"), sem("sp_turn")
        zero_ready, tables_zero, pad_ready = sem("zero_ready"), sem("tables_zero"), sem("pad_ready")
        x_in, dve_step = sem("x_in"), sem("dve_step")
        stats_ready, var_ready, std_ready, norm_ready = sem("stats_ready"), sem("var_ready"), sem("std_ready"), sem("norm_ready")
        h_ready, h_added, hT_ps, hT_sb = sem("h_ready"), sem("h_added"), sem("hT_ps"), sem("hT_sb")
        p_ps, p_sb = sem("p_ps"), sem("p_sb")
        p_out = [sem(f"p_out{i}") for i in range(2)]
        rbf_in = [sem(f"rbf_in{i}") for i in range(2)]
        idx_in = [sem(f"idx_in{i}") for i in range(2)]
        gathered = [sem(f"gathered{i}") for i in range(2)]
        scattered = [sem(f"scattered{k}") for k in range(K)]
        srcf_ready, rbfT_ps, rbfT_sb = sem("srcf_ready"), sem("rbfT_ps"), sem("rbfT_sb")
        bcast_ps, same_ready = sem("bcast_ps"), sem("same_ready")
        z_ps, z_sb, silu_ready = sem("z_ps"), sem("z_sb"), sem("silu_ready")
        sums_ps, sums_sb, rows_ready = sem("sums_ps"), sem("sums_sb"), sem("rows_ready")
        tabs_in = [sem(f"tabs_in{i}") for i in range(2)]
        pair_ready, sT_ps, sT_sb, agg_ps = sem("pair_ready"), sem("sT_ps"), sem("sT_sb"), sem("agg_ps")
        lead_step, cnt_ready, base_ready = sem("lead_step"), sem("cnt_ready"), sem("base_ready")
        out_ready = sem("out_ready")
        out_done = [sem(f"out_done{i}") for i in range(2)]

        block = ctx.enter_context(nc.Block())

        def over_groups(eng, group):
            group(0, 0, 0, G, True)
            group(1, 0, 1, G, True)
            with eng.Fori(1, GROUPS // 2) as q:
                group(q * 2, q, 0, G, False)
                group(q * 2 + 1, q, 1, G, False)
            group(GROUPS - 1, GROUPS // 2, 0, G, False)
            group(GROUPS, GROUPS // 2, 1, TT, False)

        def over_blocks(eng, step):
            step(0, 0, 0, P, True)
            step(1, 0, 1, P, True)
            with eng.Fori(1, NF // 2) as q:
                step(q * 2, q, 0, P, False)
                step(q * 2 + 1, q, 1, P, False)
            step(NB - 1, NF // 2, 0, NR, False)

        @block.sync
        def _(sp):
            xv = x[0:NF * P, :].rearrange("(b p) c -> p b c", p=P)
            for c in range(NB // CB - 1):
                sp.dma_start(xh[:, c * CB:(c + 1) * CB, :], xv[:, c * CB:(c + 1) * CB, :]).then_inc(x_in, 16)
            sp.dma_start(xh[:, NB - CB:NF, :], xv[:, NB - CB:NF, :]).then_inc(x_in, 16)
            sp.wait_ge(pad_ready, 1)
            sp.dma_start(xh[0:NR, NF, :], x[NF * P:N, :]).then_inc(x_in, 16)

            def store_p(b, q, s, n, first):
                sp.wait_ge(p_sb, b + 1)
                sp.sem_inc(sp_turn)
                sp.dma_start(p_dram[ds(b * P, n), :], prow[0:n, s, :]).then_inc(p_out[s], 16)
            over_blocks(sp, store_p)

            def load(g, q, s, tiles, first):
                tail = tiles != G
                if not first:
                    sp.wait_ge(rbfT_ps, g - 1)
                    sp.sem_inc(sp_turn)
                r = rbf_tail if tail else rbf_groups[ds(g, 1)].rearrange("a p c -> (a p) c")
                sp.dma_start(rbfs[:, s, 0:tiles * R], r).then_inc(rbf_in[s], 16)
                if not first:
                    sp.wait_ge(rows_ready, g - 1)
                    sp.sem_inc(sp_turn)
                    sp.wait_ge(gathered[s], 16 * G * q)
                    sp.sem_inc(sp_turn)
                a = src_tail if tail else src_groups[ds(g, 1)].rearrange("a p c -> (a p) c")
                b = dst_tail if tail else dst_groups[ds(g, 1)].rearrange("a p c -> (a p) c")
                sp.dma_start(srcs[:, s, 0:tiles], a).then_inc(idx_in[s], 16)
                sp.dma_start(dsts[:, s, 0:tiles], b).then_inc(idx_in[s], 16)
            over_groups(sp, load)

            for k in range(K):
                sp.wait_ge(scattered[k], 16 * (GROUPS * (G // K) + TT // K))

            def load_tables(b, q, s, n, first):
                if not first:
                    sp.wait_ge(pair_ready, b - 1)
                    sp.sem_inc(sp_turn)
                for k in range(K):
                    sp.dma_start(tabs[:, s, k, :], tables[k][ds(b * P, P), :]).then_inc(tabs_in[s], 16)

            over_blocks(sp, load_tables)

        @block.gpsimd
        def _(pool):
            steps = [0]

            def step(ins):
                steps[0] += 1
                ins.then_inc(pool_step, 1)
                pool.wait_ge(pool_step, steps[0])

            step(pool.memset(ident[:, :], 0.0))
            step(pool.affine_select(out=ident[:, :], in_=ident[:, :], compare_op=ALU.not_equal, fill=1.0,
                                    base=0, pattern=[[-1, P]], channel_multiplier=1))
            pool.iota(spare[:, :], pattern=[[0, 1]], base=N, channel_multiplier=1,
                      allow_small_or_imprecise_dtypes=True)
            step(pool.memset(bits[:, :], 0.0))
            for i in range(QB):
                step(pool.affine_select(out=bits[:, :], in_=bits[:, :], compare_op=ALU.not_equal,
                                        fill=float(1 << i), base=-i, pattern=[[-QB, Q]], channel_multiplier=1))
            step(pool.memset(belowf[:, :], 0.0))
            for i in range(1, QB):
                step(pool.affine_select(out=belowf[:, :], in_=belowf[:, :], compare_op=ALU.not_equal,
                                        fill=float((1 << i) - 1), base=-i, pattern=[[-QB, Q]],
                                        channel_multiplier=1))
            step(pool.affine_select(out=belowf[:, :], in_=belowf[:, :], compare_op=ALU.is_gt,
                                    fill=float((1 << QB) - 1), base=QB, pattern=[[QB, Q]],
                                    channel_multiplier=-1))
            step(pool.tensor_copy(below[:, :], belowf[:, :]))
            step(pool.memset(fresh[:, :], 1.0))
            step(pool.affine_select(out=fresh[:, :], in_=fresh[:, :], compare_op=ALU.is_ge, fill=0.0,
                                    base=-OLD, pattern=[[1, H]], channel_multiplier=H))
            step(pool.tensor_scalar(stale[:, :], fresh[:, :], -1.0, 1.0, ALU.mult, ALU.add))
            pool.tensor_scalar(stale[:, :], stale[:, :], spare[:, 0:1], None, ALU.mult)
            for s in range(2):
                pool.memset(act_rows[:, s, :, C + 1:W], 0.0)
                pool.memset(act_rows[:, s, :, C:C + 1], 1.0)
                for j in range(G):
                    last = pool.tensor_copy(act_rows[:, s, j, W:V], bits[:, :])
            last.then_inc(consts_done, 1)

            def add_h(b, q, s, n, first):
                pool.wait_ge(h_ready, b + 1)
                pool.tensor_tensor(xh[:, ds(b, 1), :].rearrange("p a c -> p (a c)"),
                                   xh[:, ds(b, 1), :].rearrange("p a c -> p (a c)"), hs[:, s, :],
                                   ALU.add).then_inc(h_added, 1)
            over_blocks(pool, add_h)

            pool.wait_ge(p_out[0], 16 * (NB // 2 + 1))
            pool.wait_ge(p_out[1], 16 * (NB // 2))
            pool.wait_ge(tables_zero, 32 * K)

            def edges(g, q, s, tiles, first):
                pool.wait_ge(idx_in[s], 32 * (q + 1))
                if not first:
                    pool.wait_ge(z_sb, 2 * g - 2)
                pool.sem_inc(pool_turn)
                for j in range(tiles):
                    pool.indirect_dma_start(pg[:, s, j, :], None, p_dram[:, :],
                                            bass.IndirectOffsetOnAxis(dsts[:, s, j:j + 1], 0)
                                            ).then_inc(gathered[s], 16)
                pool.wait_ge(rows_ready, g + 1)
                for j in range(tiles):
                    k = j % K
                    if not (first and s == 0 and j < K):
                        pool.wait_ge(scattered[k], 16 * (g * (G // K) + j // K))
                    pool.sem_inc(pool_turn)
                    pool.indirect_dma_start(tables[k][:, :], bass.IndirectOffsetOnAxis(rows[:, s, j:j + 1], 0),
                                            sums[:, s, j, 0:W], None, compute_op=ALU.add
                                            ).then_inc(scattered[k], 16)
            over_groups(pool, edges)

            def store(b, q, s, n, first):
                pool.wait_ge(out_ready, b + 1)
                pool.dma_start(out[ds(b * P, n), :], outs[0:n, s, :]).then_inc(out_done[s], 16)
            over_blocks(pool, store)
            pool.wait_ge(out_done[0], 16 * (NB // 2 + 1))
            pool.wait_ge(out_done[1], 16 * (NB // 2))

        @block.scalar
        def _(act):
            for i, (a, b) in enumerate((
                    (w1a[:, :, :], w1[0:C, :].rearrange("(k p) c -> p k c", p=P)),
                    (w1b[0:R, :], w1[C:C + R, :]), (w1b[R:2 * R, :], w1[C:C + R, :]),
                    (w2s[:, :, :], w2.rearrange("(k p) c -> p k c", p=P)),
                    (b1b[:, :], b1.partition_broadcast(P)), (b2b[:, :], b2.partition_broadcast(P)))):
                act.dma_start(a, b).then_inc(consts_in, 16)
            act.wait_ge(zero_ready, 1)
            for k in range(K):
                for lo in range(0, NT, ZR * P):
                    act.dma_start(tables[k][lo:lo + ZR * P, :].rearrange("(p r) w -> p (r w)", p=P),
                                  zero[:, :]).then_inc(tables_zero, 16)

            act.wait_ge(var_ready, 1)
            act.activation(rstd[:, :], mom[:, 3, :], ACT.Sqrt).then_inc(std_ready, 1)
            act.wait_ge(norm_ready, 1)

            def make_h(b, q, s, n, first):
                if not first:
                    act.wait_ge(hT_ps, b - 1)
                    act.wait_ge(h_added, b - 1)
                bb = ds(b, 1)
                act.activation(hs[:, s, :], xh[:, bb, :].rearrange("p a c -> p (a c)"), ACT.Relu,
                               bias=nmr[:, bb], scale=rstd[:, bb]).then_inc(h_ready, 1)
            over_blocks(act, make_h)

            def edges(g, q, s, tiles, first):
                act.wait_ge(rbfT_ps, g + 1)
                n = tiles // 2 * P
                if not first:
                    act.wait_ge(z_ps, 2 * g - 2)
                act.activation(rbfT[:, s, 0:n], ps_t[:, 0:tiles // 2, :].rearrange("p a b -> p (a b)"),
                               ACT.Copy).then_inc(rbfT_sb, 1)
                for h in range(tiles // H):
                    act.wait_ge(z_sb, 2 * g + h + 1)
                    if not first:
                        act.wait_ge(sums_ps, 4 * (g - 1))
                    act.activation(act_rows[:, s, h * H:(h + 1) * H, 0:C], zs[:, h, :, :],
                                   ACT.Silu).then_inc(silu_ready, 1)
            over_groups(act, edges)

            def copy_sT(b, q, s, n, first):
                act.wait_ge(sT_ps, b + 1)
                if not first:
                    act.wait_ge(agg_ps, b - 1)
                act.activation(sT[:, s, :, :], ps_t[:, 2 * s:2 * s + 2, :], ACT.Copy).then_inc(sT_sb, 1)
            over_blocks(act, copy_sT)

        @block.tensor
        def _(pe):
            pe.wait_ge(consts_done, 1)
            pe.wait_ge(consts_in, 16 * 6)

            def node(b, q, s, n, first):
                pe.wait_ge(h_ready, b + 1)
                if not first:
                    pe.wait_ge(hT_sb, b - 1)
                for k in range(KC):
                    last = pe.transpose(ps_z[:, 0, s, k * P:(k + 1) * P], hs[:, s, k * P:(k + 1) * P],
                                        ident[:, :])
                last.then_inc(hT_ps, 1)
                pe.wait_ge(hT_sb, b + 1)
                if not first:
                    pe.wait_ge(p_sb, b - 1)
                for k in range(KC):
                    last = pe.matmul(ps_z[:, 1, s, 0:C], hT[:, s, k, :], w1a[:, k, :],
                                     start=(k == 0), stop=(k == KC - 1))
                last.then_inc(p_ps, 1)
            over_blocks(pe, node)
            pe.wait_ge(p_sb, NB)

            def edges(g, q, s, tiles, first):
                pe.wait_ge(rbf_in[s], 16 * (q + 1))
                if not (first and s == 0):
                    pe.wait_ge(rbfT_sb, g)
                for i in range(tiles // 2):
                    last = pe.transpose(ps_t[:, i, :], rbfs[:, s, i * P:(i + 1) * P], ident[:, :])
                last.then_inc(rbfT_ps, 1)
                pe.wait_ge(srcf_ready, g + 1)
                pe.wait_ge(rbfT_sb, g + 1)
                for h in range(tiles // H):
                    if not (first and s == 0 and h == 0):
                        pe.wait_ge(same_ready, 2 * g + h)
                    for j in range(H):
                        last = pe.matmul(ps_b[:, j, :], srcf[:, s, h * H + j:h * H + j + 1].to_broadcast([P, P]),
                                         ident[:, :], start=True, stop=True)
                    last.then_inc(bcast_ps, 1)
                    if not (first and s == 0):
                        pe.wait_ge(z_sb, 2 * g + h - 1)
                    for i in range(H // 2):
                        for o in range(2):
                            last = pe.matmul(ps_z[:, h, o, i * C:(i + 1) * C],
                                             rbfT[o * R:(o + 1) * R, s, (h * 2 + i) * P:(h * 2 + i + 1) * P],
                                             w1b[o * R:(o + 1) * R, :], start=True, stop=True)
                    last.then_inc(z_ps, 1)
                for h in range(tiles // H):
                    pe.wait_ge(same_ready, 2 * g + h + 1)
                    pe.wait_ge(silu_ready, 2 * g + h + 1)
                    for i in range(H // 2):
                        if not (first and s == 0 and h == 0 and i == 0):
                            pe.wait_ge(sums_sb, 4 * g + 2 * h + i)
                        for o in range(2):
                            j = h * H + 2 * i + o
                            last = pe.matmul(ps_s[:, o, 0:V], same[:, h, 2 * i + o, :], act_rows[:, s, j, :],
                                             start=True, stop=True)
                        last.then_inc(sums_ps, 1)
            over_groups(pe, edges)
            pe.wait_ge(sums_sb, 4 * GROUPS + TT // 2)
            pe.wait_ge(z_sb, 2 * GROUPS + TT // H)

            def finish(b, q, s, n, first):
                pe.wait_ge(pair_ready, b + 1)
                if not first:
                    pe.wait_ge(sT_sb, b - 1)
                for k in range(KC):
                    for i in range(K // 2):
                        last = pe.matmul(ps_t[:, 2 * s + k, :], pair[:, s, i, k * P:(k + 1) * P], ident[:, :],
                                         start=(i == 0), stop=(i == K // 2 - 1))
                last.then_inc(sT_ps, 1)
                pe.wait_ge(sT_sb, b + 1)
                if not first:
                    pe.wait_ge(out_ready, b - 1)
                for k in range(KC):
                    last = pe.matmul(ps_z[:, 1, s, 0:C], sT[:, s, k, :], w2s[:, k, :],
                                     start=(k == 0), stop=(k == KC - 1))
                last.then_inc(agg_ps, 1)
            over_blocks(pe, finish)

        @block.vector
        def _(dve):
            steps = [0]

            def chain(ins):
                steps[0] += 1
                ins.then_inc(dve_step, 1)
                dve.wait_ge(dve_step, steps[0])

            dve.memset(zero[:, :], 0.0).then_inc(zero_ready, 1)
            dve.memset(xh[:, NF, :], 0.0).then_inc(pad_ready, 1)
            dve.wait_ge(x_in, 16 * (NB // CB + 1))
            with dve.Fori(0, NB // CB) as c:
                for i in range(CB):
                    b = ds(c * CB + i, 1)
                    last = dve.bn_stats(stats[:, b, :].rearrange("p a c -> p (a c)"),
                                        xh[:, b, :].rearrange("p a c -> p (a c)"))
                last.then_inc(stats_ready, 1)
            dve.wait_ge(stats_ready, NB // CB)
            me, ve, mo, vo = (stats[:, :, i] for i in (1, 2, 4, 5))
            chain(dve.tensor_tensor(mom[:, 0, :], me, mo, ALU.add))
            chain(dve.tensor_tensor(mom[:, 1, :], me, mo, ALU.subtract))
            chain(dve.tensor_tensor(mom[:, 2, :], ve, vo, ALU.add))
            chain(dve.tensor_tensor(mom[:, 1, :], mom[:, 1, :], mom[:, 1, :], ALU.mult))
            chain(dve.tensor_scalar(mom[:, 2, :], mom[:, 2, :], 1.0 / C, EPS, ALU.mult, ALU.add))
            dve.scalar_tensor_tensor(out=mom[:, 3, :], in0=mom[:, 1, :], scalar=0.25, in1=mom[:, 2, :],
                                     op0=ALU.mult, op1=ALU.add).then_inc(var_ready, 1)
            dve.wait_ge(std_ready, 1)
            chain(dve.reciprocal(rstd[:, :], rstd[:, :]))
            dve.scalar_tensor_tensor(out=nmr[:, :], in0=mom[:, 0, :], scalar=-0.5, in1=rstd[:, :],
                                     op0=ALU.mult, op1=ALU.mult).then_inc(norm_ready, 1)
            dve.wait_ge(consts_in, 16 * 6)

            def node(b, q, s, n, first):
                dve.wait_ge(hT_ps, b + 1)
                if not first:
                    dve.wait_ge(p_ps, b - 1)
                dve.tensor_copy(hT[:, s, :, :].rearrange("p k n -> p (k n)"),
                                ps_z[:, 0, s, 0:C]).then_inc(hT_sb, 1)
                dve.wait_ge(p_ps, b + 1)
                if not first:
                    dve.wait_ge(p_out[s], 16 * q)
                dve.tensor_tensor(prow[:, s, :], ps_z[:, 1, s, 0:C], b1b[:, :], ALU.add).then_inc(p_sb, 1)
            over_blocks(dve, node)

            dve.wait_ge(consts_done, 1)

            def edges(g, q, s, tiles, first):
                halves = tiles // H
                dve.wait_ge(idx_in[s], 32 * (q + 1))
                if tiles == G:
                    dve.tensor_copy(srcf[:, s, :], srcs[:, s, :]).then_inc(srcf_ready, 1)
                else:
                    chain(dve.tensor_copy(srcf[:, s, 0:tiles], srcs[:, s, 0:tiles]))
                    chain(dve.tensor_tensor(srcf[:, s, 0:tiles], srcf[:, s, 0:tiles], fresh[:, :], ALU.mult))
                    dve.tensor_tensor(srcf[:, s, 0:tiles], srcf[:, s, 0:tiles], stale[:, :],
                                      ALU.add).then_inc(srcf_ready, 1)
                dve.wait_ge(srcf_ready, g + 1)
                for h in range(halves):
                    dve.wait_ge(bcast_ps, 2 * g + h + 1)
                    if not (first and s == 0):
                        dve.wait_ge(sums_ps, 4 * g - 2 + 2 * h)
                    dve.tensor_tensor(same[:, h, :, :], ps_b[:, :, :],
                                      srcf[:, s, h * H:(h + 1) * H].unsqueeze(2).to_broadcast([P, H, P]),
                                      ALU.is_equal).then_inc(same_ready, 1)
                dve.wait_ge(gathered[s], 16 * G * q + 16 * tiles)
                for h in range(halves):
                    dve.wait_ge(z_ps, 2 * g + h + 1)
                    if not (first and s == 0):
                        dve.wait_ge(silu_ready, 2 * g + h - 1)
                    dve.tensor_tensor(zs[:, h, :, :].rearrange("p (i o) c -> p o i c", o=2),
                                      ps_z[:, h, :, :].rearrange("p o (i c) -> p o i c", c=C),
                                      pg[:, s, h * H:(h + 1) * H, :].rearrange("p (i o) c -> p o i c", o=2),
                                      ALU.add).then_inc(z_sb, 1)
                for k in range(K):
                    if not first:
                        dve.wait_ge(scattered[k], 16 * (g - 1) * (G // K))
                for i in range(tiles // 2):
                    dve.wait_ge(sums_ps, 4 * g + i + 1)
                    dve.tensor_copy(sums[:, s, 2 * i:2 * i + 2, :], ps_s[:, :, 0:V]).then_inc(sums_sb, 1)
                t = slice(0, tiles)
                n0 = 5 * g

                def link(ins, n):
                    ins.then_inc(lead_step, 1)
                    dve.wait_ge(lead_step, n0 + n)
                dve.wait_ge(sums_sb, 4 * g + tiles // 2)
                link(dve.tensor_copy(words[:, t, :], sums[:, s, t, W:V]), 1)
                link(dve.tensor_tensor(ahead[:, t, :], words[:, t, :],
                                       below[:, :].unsqueeze(1).to_broadcast([P, tiles, Q]), ALU.bitwise_and), 2)
                link(dve.tensor_reduce(anyahead[:, t], ahead[:, t, :], AX.X, ALU.max), 3)
                link(dve.tensor_scalar(leads[:, t], anyahead[:, t], 0.0, None, ALU.is_equal), 4)
                link(dve.scalar_tensor_tensor(out=shifted[:, t], in0=srcf[:, s, t], scalar=spare[:, 0:1],
                                              in1=leads[:, t], op0=ALU.subtract, op1=ALU.mult), 5)
                dve.tensor_scalar(rows[:, s, t], shifted[:, t], spare[:, 0:1], None,
                                  ALU.add).then_inc(rows_ready, 1)
            over_groups(dve, edges)
            dve.wait_ge(h_added, NB)

            def finish(b, q, s, n, first):
                dve.wait_ge(tabs_in[s], 16 * K * (q + 1))
                if not first:
                    dve.wait_ge(sT_ps, b - 1)
                dve.tensor_tensor(pair[:, s, :, :], tabs[:, s, 0:K // 2, :], tabs[:, s, K // 2:K, :],
                                  ALU.add).then_inc(pair_ready, 1)
                dve.wait_ge(pair_ready, b + 1)
                dve.tensor_tensor(cnt[:, s, :], pair[:, s, 0, C:C + 1], pair[:, s, 1, C:C + 1],
                                  ALU.add).then_inc(cnt_ready, 1)
                dve.wait_ge(cnt_ready, b + 1)
                dve.scalar_tensor_tensor(out=base[:, s, :], in0=b2b[:, :], scalar=cnt[:, s, :],
                                         in1=xh[:, ds(b, 1), :].rearrange("p a c -> p (a c)"),
                                         op0=ALU.mult, op1=ALU.add).then_inc(base_ready, 1)
                dve.wait_ge(base_ready, b + 1)
                dve.wait_ge(agg_ps, b + 1)
                if not first:
                    dve.wait_ge(out_done[s], 16 * q)
                dve.tensor_tensor(outs[:, s, :], ps_z[:, 1, s, 0:C], base[:, s, :], ALU.add).then_inc(out_ready, 1)
            over_blocks(dve, finish)


_INS = ['x', 'src', 'dst', 'edge_attr_64', 'L0_gnn_W1', 'L0_gnn_b1', 'L0_gnn_W2', 'L0_gnn_b2']
_OUTS = [((6250, 256), 'float32')]


def kernel(**inputs):
    import numpy as _np
    import concourse.bacc as _bacc
    from concourse import mybir as _mybir
    from concourse.bass_utils import run_bass_kernel_spmd as _run

    nc = _bacc.Bacc("TRN2", target_bir_lowering=False, num_devices=1)
    arrays, args = {}, []
    for name in _INS:
        a = _np.ascontiguousarray(inputs[name])
        arrays[f"in_{name}_dram"] = a
        args.append(nc.dram_tensor(f"in_{name}_dram", a.shape, _mybir.dt.from_np(a.dtype), kind="ExternalInput").ap())
    for i, (shape, dtype) in enumerate(_OUTS):
        dt = _mybir.dt.from_np(_np.dtype(dtype))
        args.append(nc.dram_tensor(f"out_{i}_dram", shape, dt, kind="ExternalOutput").ap())
    gnn_layer_kernel(nc, *args)
    r = _run(nc, [arrays], core_ids=[0])
    return r.results[0]["out_0_dram"]
```

```python
import concourse.bass as bass
from concourse import mybir
from contextlib import ExitStack

P = 128


def gnn_layer_kernel(nc, x, src, dst, rbf, w1, b1, w2, b2, out):
    F32, I32, BF16 = mybir.dt.float32, mybir.dt.int32, mybir.dt.bfloat16
    ALU, ACT, AX = mybir.AluOpType, mybir.ActivationFunctionType, mybir.AxisListType
    ds = bass.ds

    N, C = x.shape
    E, R = rbf.shape
    KC = C // P
    NB = -(-N // P)
    NF = N // P
    NR = N - NF * P
    CB = 7
    EPS = 1e-5

    G = 4
    GE = G * P
    GROUPS = -(-E // GE)
    LAST = GROUPS - 1
    OLD = GROUPS * GE - E
    GT = -(-GROUPS // P)
    GL = GROUPS - (GT - 1) * P
    WN = P - R
    assert NR > 0 and NB % CB == 0 and NB % 2 == 1 and GROUPS % 2 == 1 and 0 < OLD < GE
    K = 4
    assert K == G
    W = C + 4
    Q = 8
    QB = P // Q
    V = W + Q
    NT = (NB + 1) * P
    ZR = NT // P // 2
    FAR = 2 * P

    p_dram = nc.dram_tensor("p_rows", (NB * P, C), F32).ap()
    tables = [nc.dram_tensor(f"table{k}", (NT, W), F32).ap() for k in range(K)]
    ends_dram = nc.dram_tensor("ends", (GT * P, 2), F32).ap()
    halves_dram = nc.dram_tensor("src_halves", (GT * P, 2, GE), BF16).ap()

    rbf_groups = rbf[0:LAST * GE, :].rearrange("(g p j) r -> g p j r", p=P, j=G)
    rbf_last = rbf[E - GE:E, :].rearrange("(p j) r -> p j r", p=P)

    ctx = ExitStack()
    with ctx:
        def sb(name, shape, dt=F32):
            return ctx.enter_context(nc.sbuf_tensor(name, shape, dt))

        def ps(name, shape, dt=F32):
            return ctx.enter_context(nc.psum_tensor(name, shape, dt))

        def sem(name):
            return ctx.enter_context(nc.semaphore(name))

        def sems(name, n):
            return [sem(f"{name}{i}") for i in range(n)]

        ident = sb("ident", [P, P])
        ones2 = sb("ones2", [2, P], BF16)
        w1a = sb("w1a", [P, KC, C])
        w2s = sb("w2s", [P, KC, C])
        b1b = sb("b1b", [P, C])
        b2b = sb("b2b", [P, C])
        zero = sb("zero", [P, ZR * W])
        bits = sb("bits", [P, Q])
        belowf = sb("belowf", [P, Q])
        below = sb("below", [P, Q], I32)
        spare = sb("spare", [P, 1])
        window_col = sb("window_col", [P, WN])
        spare_row = sb("spare_row", [P, P, G])
        fresh_row = sb("fresh_row", [P, GE])
        stale_row = sb("stale_row", [P, GE])
        xh = sb("xh", [P, NB, C])
        stats = sb("stats", [P, NB, 6])
        mom = sb("mom", [P, 4, NB])
        rstd = sb("rstd", [P, NB])
        nmr = sb("nmr", [P, NB])
        hs = sb("hs", [P, 2, C])
        hT = sb("hT", [P, 2, KC, P])
        prow = sb("prow", [P, 2, C])
        src_rows = sb("src_rows", [P, GT, GE], I32)
        dst_rows = sb("dst_rows", [P, GT, GE], I32)
        src_f = sb("src_f", [P, GT, GE])
        dst_f = sb("dst_f", [P, GT, GE])
        low = dst_f[:, :, :].bitcast(I32)
        halves = sb("halves", [P, GT, 2, GE], BF16)
        least = sb("least", [P, GT])
        most = sb("most", [P, GT])
        ends = sb("ends_sb", [P, GT, 2])
        moved = sb("moved", [P, GT])
        all_ends = sb("all_ends", [P, GT * P, 2])
        base_words = sb("base_words", [1, GT * P], I32)
        widest = sb("widest", [P, 1])
        windowed = sb("windowed", [P, 1])
        general = sb("general", [P, 1], I32)
        src_cols = sb("src_cols", [P, GT * P * G])
        dst_cols = sb("dst_cols", [P, GT * P * G])
        lead_cols = sb("lead_cols", [P, GT * P * G])
        feats = sb("feats", [P, 2, G, R + WN])
        lhs = sb("lhs", [P, 2, GE])
        rhs = sb("rhs", [P, 2, C])
        src_line = sb("src_line", [2, 2, GE], BF16)
        act_rows = sb("act_rows", [P, 2, G, V])
        same = sb("same", [P, 2, G, P])
        sums = sb("sums", [P, 2, G, V])
        words = sb("words", [P, G, Q], I32)
        ahead = sb("ahead", [P, G, Q], I32)
        any_ahead = sb("any_ahead", [P, G])
        shifted = sb("shifted", [P, G])
        rows = sb("rows", [P, 2, G], I32)
        dst_index = sb("dst_index", [P, 2, G], I32)
        slots = 2 * G * C
        assert 2 * slots + 2 * K * W <= ZR * W
        gathered_rows = zero[:, 0:slots].rearrange("p (s j c) -> p s j c", s=2, j=G)
        pre = zero[:, slots:2 * slots].rearrange("p (s j c) -> p s j c", s=2, j=G)
        tabs = zero[:, 2 * slots:2 * slots + 2 * K * W].rearrange("p (s k w) -> p s k w", s=2, k=K)
        pair = sb("pair", [P, 2, K // 2, W])
        cnt = sb("cnt", [P, 2, 1])
        sT, base, outs = hT, hs, prow

        ps_t = ps("ps_t", [P, G, P])
        ps_b = ps("ps_b", [P, G, P])
        ps_z = ps("ps_z", [P, G, C])
        ps_s = ps("ps_s", [P, G, 512])

        consts_in, consts_done, pool_step = sem("consts_in"), sem("consts_done"), sem("pool_step")
        pool_turn, sp_turn, dve_step, dve_misc = sem("pool_turn"), sem("sp_turn"), sem("dve_step"), sem("dve_misc")
        zero_ready, tables_zero, pad_ready = sem("zero_ready"), sem("tables_zero"), sem("pad_ready")
        rows_clear, ends_in, ends_ready, ends_out = sem("rows_clear"), sem("ends_in"), sem("ends_ready"), sem("ends_out")
        spans_in, general_ready, halves_ready, halves_out = (
            sem("spans_in"), sem("general_ready"), sem("halves_ready"), sem("halves_out"))
        line_ready, cols_ps, cols_sb = sem("line_ready"), sem("cols_ps"), sem("cols_sb")
        x_in, stats_ready = sem("x_in"), sem("stats_ready")
        var_ready, std_ready, norm_ready = sem("var_ready"), sem("std_ready"), sem("norm_ready")
        h_ready, h_added, hT_ps, hT_sb = sem("h_ready"), sem("h_added"), sem("hT_ps"), sem("hT_sb")
        p_ps, p_sb, p_out = sem("p_ps"), sem("p_sb"), sems("p_out", 2)
        rbf_in, window_in, line_in = sems("rbf_in", 2), sems("window_in", 2), sems("line_in", 2)
        onehot_ready, lhs_ps, lhs_sb = sem("onehot_ready"), sem("lhs_ps"), sem("lhs_sb")
        z_ps, silu_ready, bcast_ps, same_ready = sem("z_ps"), sem("silu_ready"), sem("bcast_ps"), sem("same_ready")
        sums_ps, sums_sb, lead_step, rows_ready = sem("sums_ps"), sem("sums_sb"), sem("lead_step"), sem("rows_ready")
        scattered = sems("scattered", K)
        index_ready, gathered, pre_ready = sem("index_ready"), sems("gathered", 2), sem("pre_ready")
        tabs_in, out_done = sems("tabs_in", 2), sems("out_done", 2)
        pair_ready, sT_ps, sT_sb, agg_ps = sem("pair_ready"), sem("sT_ps"), sem("sT_sb"), sem("agg_ps")
        cnt_ready, base_ready, out_ready = sem("cnt_ready"), sem("base_ready"), sem("out_ready")

        block = ctx.enter_context(nc.Block())

        def over_blocks(eng, step):
            step(0, 0, 0, P, True)
            step(1, 0, 1, P, True)
            with eng.Fori(1, NF // 2) as q:
                step(q * 2, q, 0, P, False)
                step(q * 2 + 1, q, 1, P, False)
            step(NB - 1, NF // 2, 0, NR, False)

        def over_turns(eng, turn):
            turn(0, 0, 0)
            turn(1, 0, 1)
            with eng.Fori(1, LAST // 2 - 1) as q:
                turn(q * 2, q, 0)
                turn(q * 2 + 1, q, 1)
            for t in range(LAST - 2, LAST + 2):
                turn(t, t // 2, t % 2)

        def known(t):
            return isinstance(t, int)

        def exists(g):
            return not known(g) or 0 <= g <= LAST

        def before(g):
            return not known(g) or g >= 2

        @block.sync
        def _(sp):
            sp.wait_ge(rows_clear, 2)
            full = (GT - 1) * P
            for rows_, ends_ in ((src_rows, src), (dst_rows, dst)):
                sp.dma_start(rows_[:, 0:GT - 1, :],
                             ends_[0:full * GE].rearrange("(t r c) -> r t c", r=P, c=GE)).then_inc(ends_in, 16)
                sp.dma_start(rows_[0:GL - 1, GT - 1, :],
                             ends_[full * GE:LAST * GE].rearrange("(r c) -> r c", c=GE)).then_inc(ends_in, 16)
                sp.dma_start(rows_[GL - 1:GL, GT - 1, :],
                             ends_[E - GE:E].rearrange("(a c) -> a c", a=1)).then_inc(ends_in, 16)
            xv = x[0:NF * P, :].rearrange("(b p) c -> p b c", p=P)
            for c in range(NB // CB - 1):
                sp.dma_start(xh[:, c * CB:(c + 1) * CB, :], xv[:, c * CB:(c + 1) * CB, :]).then_inc(x_in, 16)
            sp.dma_start(xh[:, NB - CB:NF, :], xv[:, NB - CB:NF, :]).then_inc(x_in, 16)
            sp.wait_ge(pad_ready, 1)
            sp.dma_start(xh[0:NR, NF, :], x[NF * P:N, :]).then_inc(x_in, 16)

            sp.wait_ge(ends_ready, 1)
            sp.dma_start(ends_dram.rearrange("(t r) k -> r t k", r=P), ends[:, :, :]).then_inc(ends_out, 16)
            sp.wait_ge(ends_out, 16)
            sp.dma_start(all_ends[:, :, :].rearrange("p g k -> p (g k)"),
                         ends_dram.rearrange("g k -> (g k)").partition_broadcast(P)).then_inc(spans_in, 16)
            sp.wait_ge(halves_ready, 2)
            sp.dma_start(halves_dram.rearrange("(t r) h c -> r t h c", r=P), halves[:, :, :, :]).then_inc(halves_out, 16)

            def store_p(b, q, s, n, first):
                sp.wait_ge(p_sb, b + 1)
                sp.sem_inc(sp_turn)
                sp.dma_start(p_dram[ds(b * P, P), :], prow[:, s, :]).then_inc(p_out[s], 16)
            over_blocks(sp, store_p)
            sp.wait_ge(halves_out, 16)
            sp.wait_ge(p_out[0], 16 * (NB // 2 + 1))
            sp.wait_ge(p_out[1], 16 * (NB // 2))
            sp.wait_ge(line_ready, 1)

            def load_rbf(g, q, s):
                if before(g):
                    sp.wait_ge(lhs_ps, g - 1)
                    sp.sem_inc(sp_turn)
                r = rbf_last if known(g) and g == LAST else rbf_groups[ds(g, 1)].rearrange("a p j r -> (a p) j r")
                sp.dma_start(feats[:, s, :, 0:R], r).then_inc(rbf_in[s], 16)

            def load_window(g, q, s):
                if before(g):
                    sp.wait_ge(z_ps, g - 1)
                    sp.sem_inc(sp_turn)
                first = sp.value_load(base_words[0:1, ds(g, 1)], min_val=0, max_val=NB * P - WN)
                sp.dma_start(rhs[R:P, s, :], p_dram[ds(first, WN), :]).then_inc(window_in[s], 16)

            def load_line(g, q, s):
                if before(g):
                    sp.wait_ge(bcast_ps, g - 1)
                    sp.sem_inc(sp_turn)
                sp.dma_start(src_line[:, s, :], halves_dram[ds(g, 1)].rearrange("a h c -> (a h) c")
                             ).then_inc(line_in[s], 16)

            def loads(t, q, s):
                if known(t) and t == 0:
                    load_rbf(0, 0, 0)
                if exists(t + 1):
                    load_rbf(t + 1, q + s, 1 - s)
                if exists(t):
                    load_window(t, q, s)
                    load_line(t, q, s)
            over_turns(sp, loads)

            for k in range(K):
                sp.wait_ge(scattered[k], 16 * GROUPS)

            def load_tables(b, q, s, n, first):
                if not first:
                    sp.wait_ge(pair_ready, b - 1)
                    sp.sem_inc(sp_turn)
                for k in range(K):
                    sp.dma_start(tabs[:, s, k, :], tables[k][ds(b * P, P), :]).then_inc(tabs_in[s], 16)
            over_blocks(sp, load_tables)

        @block.gpsimd
        def _(pool):
            steps = [0]

            def step(ins):
                steps[0] += 1
                ins.then_inc(pool_step, 1)
                pool.wait_ge(pool_step, steps[0])

            step(pool.memset(ident[:, :], 0.0))
            step(pool.affine_select(out=ident[:, :], in_=ident[:, :], compare_op=ALU.not_equal, fill=1.0,
                                    base=0, pattern=[[-1, P]], channel_multiplier=1))
            pool.memset(ones2[:, :], 1.0)
            pool.iota(window_col[:, :], pattern=[[1, WN]], base=0, channel_multiplier=0,
                      allow_small_or_imprecise_dtypes=True)
            pool.iota(spare_row[:, :, :], pattern=[[1, P], [0, G]], base=N, channel_multiplier=0,
                      allow_small_or_imprecise_dtypes=True)
            step(pool.memset(stale_row[:, :], 0.0))
            step(pool.affine_select(out=stale_row[:, :], in_=stale_row[:, :], compare_op=ALU.not_equal,
                                    fill=1.0, base=-(GL - 1), pattern=[[0, GE]], channel_multiplier=1))
            step(pool.affine_select(out=stale_row[:, :], in_=stale_row[:, :], compare_op=ALU.is_gt,
                                    fill=0.0, base=OLD, pattern=[[-1, GE]], channel_multiplier=0))
            step(pool.tensor_scalar(fresh_row[:, :], stale_row[:, :], -1.0, 1.0, ALU.mult, ALU.add))
            step(pool.tensor_tensor(stale_row[:, :], stale_row[:, :],
                                    spare_row[:, :, :].rearrange("p a b -> p (a b)"), ALU.mult))
            pool.iota(spare[:, :], pattern=[[0, 1]], base=N, channel_multiplier=1,
                      allow_small_or_imprecise_dtypes=True).then_inc(consts_done, 1)
            step(pool.memset(bits[:, :], 0.0))
            for i in range(QB):
                step(pool.affine_select(out=bits[:, :], in_=bits[:, :], compare_op=ALU.not_equal,
                                        fill=float(1 << i), base=-i, pattern=[[-QB, Q]], channel_multiplier=1))
            step(pool.memset(belowf[:, :], 0.0))
            for i in range(1, QB):
                step(pool.affine_select(out=belowf[:, :], in_=belowf[:, :], compare_op=ALU.not_equal,
                                        fill=float((1 << i) - 1), base=-i, pattern=[[-QB, Q]],
                                        channel_multiplier=1))
            step(pool.affine_select(out=belowf[:, :], in_=belowf[:, :], compare_op=ALU.is_gt,
                                    fill=float((1 << QB) - 1), base=QB, pattern=[[QB, Q]],
                                    channel_multiplier=-1))
            step(pool.tensor_copy(below[:, :], belowf[:, :]))
            for s in range(2):
                pool.memset(act_rows[:, s, :, C + 1:W], 0.0)
                pool.memset(act_rows[:, s, :, C:C + 1], 1.0)
                for j in range(G):
                    last = pool.tensor_copy(act_rows[:, s, j, W:V], bits[:, :])
            last.then_inc(consts_done, 1)

            def add_h(b, q, s, n, first):
                pool.wait_ge(h_ready, b + 1)
                pool.tensor_tensor(xh[:, ds(b, 1), :].rearrange("p a c -> p (a c)"),
                                   xh[:, ds(b, 1), :].rearrange("p a c -> p (a c)"), hs[:, s, :],
                                   ALU.add).then_inc(h_added, 1)
            over_blocks(pool, add_h)

            def scatter(g, q, s):
                pool.wait_ge(rows_ready, g + 1)
                pool.sem_inc(pool_turn)
                for j in range(G):
                    if not (known(g) and g == 0):
                        pool.wait_ge(scattered[j], 16 * g)
                        pool.sem_inc(pool_turn)
                    pool.indirect_dma_start(tables[j][:, :], bass.IndirectOffsetOnAxis(rows[:, s, j:j + 1], 0),
                                            sums[:, s, j, 0:W], None, compute_op=ALU.add
                                            ).then_inc(scattered[j], 16)

            def gather(g, q, s):
                pool.wait_ge(index_ready, g + 1)
                if before(g):
                    pool.sem_inc(pool_turn)
                    pool.wait_ge(pre_ready, g - 1)
                pool.sem_inc(pool_turn)
                for j in range(G):
                    pool.indirect_dma_start(gathered_rows[:, s, j, :], None, p_dram[:, :],
                                            bass.IndirectOffsetOnAxis(dst_index[:, s, j:j + 1], 0)
                                            ).then_inc(gathered[s], 16)

            pool.wait_ge(tables_zero, 16 * K * NT // (ZR * P))
            pool.wait_ge(p_out[0], 16 * (NB // 2 + 1))
            pool.wait_ge(p_out[1], 16 * (NB // 2))
            pool.wait_ge(general_ready, 1)
            flag = pool.value_load(general[0:1, 0:1], min_val=0, max_val=1)
            with pool.If(flag):
                def with_gather(t, q, s):
                    if exists(t):
                        gather(t, q, s)
                    if exists(t - 1):
                        scatter(t - 1, q - 1 + s, 1 - s)
                over_turns(pool, with_gather)
            with pool.Else():
                def scatter_only(t, q, s):
                    if exists(t - 1):
                        scatter(t - 1, q - 1 + s, 1 - s)
                over_turns(pool, scatter_only)

            def store(b, q, s, n, first):
                pool.wait_ge(out_ready, b + 1)
                pool.dma_start(out[ds(b * P, n), :], outs[0:n, s, :]).then_inc(out_done[s], 16)
            over_blocks(pool, store)
            pool.wait_ge(out_done[0], 16 * (NB // 2 + 1))
            pool.wait_ge(out_done[1], 16 * (NB // 2))

        @block.scalar
        def _(act):
            for a, b in ((w1a[:, :, :], w1[0:C, :].rearrange("(k p) c -> p k c", p=P)),
                         (rhs[0:R, 0, :], w1[C:C + R, :]), (rhs[0:R, 1, :], w1[C:C + R, :]),
                         (w2s[:, :, :], w2.rearrange("(k p) c -> p k c", p=P)),
                         (b1b[:, :], b1.partition_broadcast(P)), (b2b[:, :], b2.partition_broadcast(P))):
                act.dma_start(a, b).then_inc(consts_in, 16)
            act.wait_ge(x_in, 16 * (NB // CB + 1))
            act.wait_ge(zero_ready, 1)
            for k in range(K):
                for lo in range(0, NT, ZR * P):
                    act.dma_start(tables[k][lo:lo + ZR * P, :].rearrange("(p r) w -> p (r w)", p=P),
                                  zero[:, :]).then_inc(tables_zero, 16)

            act.wait_ge(var_ready, 1)
            act.activation(rstd[:, :], mom[:, 3, :], ACT.Sqrt).then_inc(std_ready, 1)
            act.wait_ge(norm_ready, 1)

            def make_h(b, q, s, n, first):
                if not first:
                    act.wait_ge(hT_ps, b - 1)
                    act.wait_ge(h_added, b - 1)
                bb = ds(b, 1)
                act.activation(hs[:, s, :], xh[:, bb, :].rearrange("p a c -> p (a c)"), ACT.Relu,
                               bias=nmr[:, bb], scale=rstd[:, bb]).then_inc(h_ready, 1)
            over_blocks(act, make_h)

            def copy_lhs(g, q, s):
                act.wait_ge(lhs_ps, g + 1)
                if before(g):
                    act.wait_ge(z_ps, g - 1)
                act.activation(lhs[:, s, :], ps_t[:, :, :].rearrange("p a b -> p (a b)"),
                               ACT.Copy).then_inc(lhs_sb, 1)

            def silu(g, q, s, gathers):
                act.wait_ge(pre_ready if gathers else z_ps, g + 1)
                if before(g):
                    act.wait_ge(sums_ps, 2 * g - 2)
                act.activation(act_rows[:, s, :, 0:C], pre[:, s, :, :] if gathers else ps_z[:, :, :],
                               ACT.Silu).then_inc(silu_ready, 1)

            def turns(gathers):
                def turn(t, q, s):
                    if known(t) and t == 0:
                        copy_lhs(0, 0, 0)
                    if exists(t + 1):
                        copy_lhs(t + 1, q + s, 1 - s)
                    if exists(t):
                        silu(t, q, s, gathers)
                over_turns(act, turn)

            act.wait_ge(consts_done, 2)
            act.wait_ge(general_ready, 1)
            flag = act.value_load(general[0:1, 0:1], min_val=0, max_val=1)
            with act.If(flag):
                turns(True)
            with act.Else():
                turns(False)

            def copy_sT(b, q, s, n, first):
                act.wait_ge(sT_ps, b + 1)
                if not first:
                    act.wait_ge(agg_ps, b - 1)
                act.activation(sT[:, s, :, :], ps_t[:, 2 * s:2 * s + 2, :], ACT.Copy).then_inc(sT_sb, 1)
            over_blocks(act, copy_sT)

        @block.tensor
        def _(pe):
            pe.wait_ge(consts_done, 1)
            pe.wait_ge(consts_in, 16 * 6)
            for n, (rows_, t) in enumerate([(r, t) for r in (src_f, dst_f) for t in range(GT)]):
                if t == 0:
                    pe.wait_ge(halves_ready if rows_ is src_f else line_ready, 1)
                if n >= 2:
                    pe.wait_ge(cols_sb, n - 1)
                bank = (ps_t, ps_b)[n % 2]
                for j in range(G):
                    last = pe.transpose(bank[:, j, :], rows_[:, t, :].rearrange("r (p j) -> r j p", j=G)[:, j, :],
                                        ident[:, :])
                last.then_inc(cols_ps, 1)

            def node(b, q, s, n, first):
                pe.wait_ge(h_ready, b + 1)
                if not first:
                    pe.wait_ge(hT_sb, b - 1)
                for k in range(KC):
                    last = pe.transpose(ps_s[:, s, k * P:(k + 1) * P], hs[:, s, k * P:(k + 1) * P], ident[:, :])
                last.then_inc(hT_ps, 1)
                pe.wait_ge(hT_sb, b + 1)
                if not first:
                    pe.wait_ge(p_sb, b - 1)
                for k in range(KC):
                    last = pe.matmul(ps_s[:, 2 + s, 0:C], hT[:, s, k, :], w1a[:, k, :],
                                     start=(k == 0), stop=(k == KC - 1))
                last.then_inc(p_ps, 1)
            over_blocks(pe, node)
            pe.wait_ge(p_sb, NB)
            pe.wait_ge(cols_sb, 2 * GT)
            pe.wait_ge(consts_done, 2)

            def transpose(g, q, s):
                pe.wait_ge(rbf_in[s], 16 * (q + 1))
                pe.wait_ge(onehot_ready, g + 1)
                if not (known(g) and g == 0):
                    pe.wait_ge(lhs_sb, g)
                for j in range(G):
                    last = pe.transpose(ps_t[:, j, :], feats[:, s, j, :], ident[:, :])
                last.then_inc(lhs_ps, 1)

            def product(g, q, s):
                pe.wait_ge(lhs_sb, g + 1)
                pe.wait_ge(window_in[s], 16 * (q + 1))
                if not (known(g) and g == 0):
                    pe.wait_ge(silu_ready, g)
                for j in range(G):
                    last = pe.matmul(ps_z[:, j, :], lhs[:, s, j * P:(j + 1) * P], rhs[:, s, :],
                                     start=True, stop=True)
                last.then_inc(z_ps, 1)

            def broadcast(g, q, s):
                pe.wait_ge(line_in[s], 16 * (q + 1))
                if not (known(g) and g == 0):
                    pe.wait_ge(same_ready, g)
                pe.matmul(ps_b[:, :, :].rearrange("p a b -> p (a b)"), ones2[:, :], src_line[:, s, :],
                          start=True, stop=True).then_inc(bcast_ps, 1)

            def sum_same(g, q, s):
                pe.wait_ge(silu_ready, g + 1)
                pe.wait_ge(same_ready, g + 1)
                for j in range(G):
                    if j % 2 == 0 and not (known(g) and g == 0):
                        pe.wait_ge(sums_sb, 2 * g + j // 2 - 1)
                    last = pe.matmul(ps_s[:, j, 0:V], same[:, s, j, :], act_rows[:, s, j, :],
                                     start=True, stop=True)
                    if j % 2 == 1:
                        last.then_inc(sums_ps, 1)

            def turn(t, q, s):
                if known(t) and t == 0:
                    transpose(0, 0, 0)
                if exists(t + 1):
                    transpose(t + 1, q + s, 1 - s)
                if exists(t):
                    product(t, q, s)
                    broadcast(t, q, s)
                if exists(t - 1):
                    sum_same(t - 1, q - 1 + s, 1 - s)
            over_turns(pe, turn)
            pe.wait_ge(sums_sb, 2 * GROUPS)

            def finish(b, q, s, n, first):
                pe.wait_ge(pair_ready, b + 1)
                if not first:
                    pe.wait_ge(sT_sb, b - 1)
                for k in range(KC):
                    for i in range(K // 2):
                        last = pe.matmul(ps_t[:, 2 * s + k, :], pair[:, s, i, k * P:(k + 1) * P], ident[:, :],
                                         start=(i == 0), stop=(i == K // 2 - 1))
                last.then_inc(sT_ps, 1)
                pe.wait_ge(sT_sb, b + 1)
                if not first:
                    pe.wait_ge(out_ready, b - 1)
                for k in range(KC):
                    last = pe.matmul(ps_s[:, s, 0:C], sT[:, s, k, :], w2s[:, k, :],
                                     start=(k == 0), stop=(k == KC - 1))
                last.then_inc(agg_ps, 1)
            over_blocks(pe, finish)

        @block.vector
        def _(dve):
            steps = [0]

            def chain(ins):
                steps[0] += 1
                ins.then_inc(dve_step, 1)
                dve.wait_ge(dve_step, steps[0])

            dve.memset(src_rows[:, GT - 1, :], 0).then_inc(rows_clear, 1)
            dve.memset(dst_rows[:, GT - 1, :], 0).then_inc(rows_clear, 1)
            dve.memset(xh[:, NF, :], 0.0).then_inc(pad_ready, 1)
            dve.memset(zero[:, :], 0.0).then_inc(zero_ready, 1)

            dve.wait_ge(ends_in, 16 * 6)
            dve.tensor_reduce(least[:, :], dst_rows[:, :, :], AX.X, ALU.min)
            chain(dve.tensor_reduce(most[:, :], dst_rows[:, :, :], AX.X, ALU.max))
            chain(dve.tensor_scalar(ends[:, :, 0], least[:, :], float(NB * P - WN), None, ALU.min))
            dve.tensor_tensor(ends[:, :, 1], most[:, :], ends[:, :, 0], ALU.subtract).then_inc(ends_ready, 1)

            chain(dve.tensor_copy(src_f[:, :, :], src_rows[:, :, :]))
            dve.wait_ge(consts_done, 1)
            tail = src_f[:, GT - 1, :]
            chain(dve.tensor_tensor(tail, tail, fresh_row[:, :], ALU.mult))
            chain(dve.tensor_tensor(tail, tail, stale_row[:, :], ALU.add))
            chain(dve.tensor_copy(src_rows[:, GT - 1, :], tail))
            chain(dve.tensor_scalar(low, src_rows[:, :, :], 255, None, ALU.bitwise_and))
            by_tile = "r t (p j) -> r t j p"
            for t in range(GT):
                view = halves[:, t, 1, :].rearrange("r (j p) -> r j p", j=G)
                lo = low[:, t, :].rearrange("r (p j) -> r j p", j=G)
                dve.tensor_copy(view, lo)
                view = halves[:, t, 0, :].rearrange("r (j p) -> r j p", j=G)
                last = dve.tensor_tensor(view, src_f[:, t, :].rearrange("r (p j) -> r j p", j=G), lo, ALU.subtract)
            last.then_inc(halves_ready, 1)
            dve.wait_ge(halves_ready, 1)
            dve.sem_inc(halves_ready)

            dve.wait_ge(spans_in, 16)
            dve.tensor_copy(base_words[:, :], all_ends[0:1, :, 0])
            chain(dve.tensor_reduce(widest[:, :], all_ends[:, :, 1], AX.X, ALU.max))
            chain(dve.tensor_scalar(windowed[:, :], widest[:, :], float(WN), None, ALU.is_lt))
            dve.tensor_scalar(general[:, :], windowed[:, :], -1.0, 1.0, ALU.mult, ALU.add).then_inc(general_ready, 1)
            chain(dve.tensor_scalar(moved[:, :], ends[:, :, 0], float(FAR), windowed[:, 0:1], ALU.add, ALU.mult))
            chain(dve.tensor_scalar(moved[:, :], moved[:, :], float(-FAR), None, ALU.add))
            for t in range(GT):
                last = dve.tensor_scalar(dst_f[:, t, :], dst_rows[:, t, :], moved[:, t:t + 1], None, ALU.subtract)
            last.then_inc(line_ready, 1)

            for n in range(2 * GT):
                dve.wait_ge(cols_ps, n + 1)
                cols = (src_cols, dst_cols)[n // GT]
                t = n % GT
                dve.tensor_copy(cols[:, t * P * G:(t + 1) * P * G].rearrange("p (g j) -> p j g", j=G),
                                (ps_t, ps_b)[n % 2][:, :, :]).then_inc(cols_sb, 1)
            dve.wait_ge(cols_sb, 2 * GT)
            chain(dve.tensor_scalar(lead_cols[:, :], src_cols[:, :], spare[:, 0:1], None, ALU.subtract))

            dve.wait_ge(x_in, 16 * (NB // CB + 1))
            with dve.Fori(0, NB // CB) as c:
                for i in range(CB):
                    b = ds(c * CB + i, 1)
                    last = dve.bn_stats(stats[:, b, :].rearrange("p a c -> p (a c)"),
                                        xh[:, b, :].rearrange("p a c -> p (a c)"))
                last.then_inc(stats_ready, 1)
            dve.wait_ge(stats_ready, NB // CB)
            me, ve, mo, vo = (stats[:, :, i] for i in (1, 2, 4, 5))
            chain(dve.tensor_tensor(mom[:, 0, :], me, mo, ALU.add))
            chain(dve.tensor_tensor(mom[:, 1, :], me, mo, ALU.subtract))
            chain(dve.tensor_tensor(mom[:, 2, :], ve, vo, ALU.add))
            chain(dve.tensor_tensor(mom[:, 1, :], mom[:, 1, :], mom[:, 1, :], ALU.mult))
            chain(dve.tensor_scalar(mom[:, 2, :], mom[:, 2, :], 1.0 / C, EPS, ALU.mult, ALU.add))
            dve.scalar_tensor_tensor(out=mom[:, 3, :], in0=mom[:, 1, :], scalar=0.25, in1=mom[:, 2, :],
                                     op0=ALU.mult, op1=ALU.add).then_inc(var_ready, 1)
            dve.wait_ge(std_ready, 1)
            chain(dve.reciprocal(rstd[:, :], rstd[:, :]))
            dve.scalar_tensor_tensor(out=nmr[:, :], in0=mom[:, 0, :], scalar=-0.5, in1=rstd[:, :],
                                     op0=ALU.mult, op1=ALU.mult).then_inc(norm_ready, 1)
            dve.wait_ge(consts_in, 16 * 6)

            def node(b, q, s, n, first):
                dve.wait_ge(hT_ps, b + 1)
                if not first:
                    dve.wait_ge(p_ps, b - 1)
                dve.tensor_copy(hT[:, s, :, :].rearrange("p k n -> p (k n)"),
                                ps_s[:, s, 0:C]).then_inc(hT_sb, 1)
                dve.wait_ge(p_ps, b + 1)
                if not first:
                    dve.wait_ge(p_out[s], 16 * q)
                dve.tensor_tensor(prow[:, s, :], ps_s[:, 2 + s, 0:C], b1b[:, :], ALU.add).then_inc(p_sb, 1)
            over_blocks(dve, node)

            dve.wait_ge(consts_done, 2)

            def onehot(g, q, s):
                if before(g):
                    dve.wait_ge(lhs_ps, g - 1)
                dve.tensor_tensor(feats[:, s, :, R:R + WN],
                                  window_col[:, :].unsqueeze(1).to_broadcast([P, G, WN]),
                                  dst_cols[:, ds(g * G, G)].unsqueeze(2).to_broadcast([P, G, WN]),
                                  ALU.is_equal).then_inc(onehot_ready, 1)

            def equal_src(g, q, s):
                dve.wait_ge(bcast_ps, g + 1)
                if before(g):
                    dve.wait_ge(sums_ps, 2 * g - 2)
                dve.tensor_tensor(same[:, s, :, :], ps_b[:, :, :],
                                  src_cols[:, ds(g * G, G)].unsqueeze(2).to_broadcast([P, G, P]),
                                  ALU.is_equal).then_inc(same_ready, 1)

            def copy_sums(g, q, s):
                if before(g):
                    for k in range(K):
                        dve.wait_ge(scattered[k], 16 * (g - 1))
                for i in range(2):
                    dve.wait_ge(sums_ps, 2 * g + i + 1)
                    dve.tensor_copy(sums[:, s, 2 * i:2 * i + 2, :],
                                    ps_s[:, 2 * i:2 * i + 2, 0:V]).then_inc(sums_sb, 1)

            def leading_rows(g, q, s):
                def link(ins, n):
                    ins.then_inc(lead_step, 1)
                    dve.wait_ge(lead_step, 4 * g + n)
                dve.wait_ge(sums_sb, 2 * g + 2)
                link(dve.tensor_copy(words[:, :, :], sums[:, s, :, W:V]), 1)
                link(dve.tensor_tensor(ahead[:, :, :], words[:, :, :],
                                       below[:, :].unsqueeze(1).to_broadcast([P, G, Q]), ALU.bitwise_and), 2)
                link(dve.tensor_reduce(any_ahead[:, :], ahead[:, :, :], AX.X, ALU.max), 3)
                link(dve.scalar_tensor_tensor(out=shifted[:, :], in0=any_ahead[:, :], scalar=0.0,
                                              in1=lead_cols[:, ds(g * G, G)], op0=ALU.is_equal, op1=ALU.mult), 4)
                dve.tensor_scalar(rows[:, s, :], shifted[:, :], spare[:, 0:1], None, ALU.add).then_inc(rows_ready, 1)

            def index(g, q, s):
                dve.tensor_scalar(dst_index[:, s, :], dst_cols[:, ds(g * G, G)], float(-FAR), None,
                                  ALU.add).then_inc(index_ready, 1)

            def add_gathered(g, q, s):
                dve.wait_ge(gathered[s], 16 * G * (q + 1))
                dve.wait_ge(z_ps, g + 1)
                if before(g):
                    dve.wait_ge(silu_ready, g - 1)
                dve.tensor_tensor(pre[:, s, :, :], ps_z[:, :, :], gathered_rows[:, s, :, :],
                                  ALU.add).then_inc(pre_ready, 1)

            def turns(gathers):
                def turn(t, q, s):
                    if known(t) and t == 0:
                        onehot(0, 0, 0)
                        onehot(1, 0, 1)
                        if gathers:
                            index(0, 0, 0)
                    if gathers and exists(t + 1):
                        index(t + 1, q + s, 1 - s)
                    if exists(t + 2):
                        onehot(t + 2, q + 1, s)
                    if exists(t):
                        equal_src(t, q, s)
                    if exists(t - 1):
                        copy_sums(t - 1, q - 1 + s, 1 - s)
                        leading_rows(t - 1, q - 1 + s, 1 - s)
                    if gathers and exists(t):
                        add_gathered(t, q, s)
                over_turns(dve, turn)

            flag = dve.value_load(general[0:1, 0:1], min_val=0, max_val=1)
            with dve.If(flag):
                turns(True)
            with dve.Else():
                turns(False)
            dve.wait_ge(h_added, NB)

            def finish(b, q, s, n, first):
                dve.wait_ge(tabs_in[s], 16 * K * (q + 1))
                if not first:
                    dve.wait_ge(sT_ps, b - 1)
                dve.tensor_tensor(pair[:, s, :, :], tabs[:, s, 0:K // 2, :], tabs[:, s, K // 2:K, :],
                                  ALU.add).then_inc(pair_ready, 1)
                dve.wait_ge(pair_ready, b + 1)
                dve.tensor_tensor(cnt[:, s, :], pair[:, s, 0, C:C + 1], pair[:, s, 1, C:C + 1],
                                  ALU.add).then_inc(cnt_ready, 1)
                dve.wait_ge(cnt_ready, b + 1)
                dve.scalar_tensor_tensor(out=base[:, s, :], in0=b2b[:, :], scalar=cnt[:, s, :],
                                         in1=xh[:, ds(b, 1), :].rearrange("p a c -> p (a c)"),
                                         op0=ALU.mult, op1=ALU.add).then_inc(base_ready, 1)
                dve.wait_ge(base_ready, b + 1)
                dve.wait_ge(agg_ps, b + 1)
                if not first:
                    dve.wait_ge(out_done[s], 16 * q)
                dve.tensor_tensor(outs[:, s, :], ps_s[:, s, 0:C], base[:, s, :], ALU.add).then_inc(out_ready, 1)
            over_blocks(dve, finish)


_INS = ['x', 'src', 'dst', 'edge_attr_64', 'L0_gnn_W1', 'L0_gnn_b1', 'L0_gnn_W2', 'L0_gnn_b2']
_OUTS = [((6250, 256), 'float32')]


def kernel(**inputs):
    import numpy as _np
    import concourse.bacc as _bacc
    from concourse import mybir as _mybir
    from concourse.bass_utils import run_bass_kernel_spmd as _run

    nc = _bacc.Bacc("TRN2", target_bir_lowering=False, num_devices=1)
    arrays, args = {}, []
    for name in _INS:
        a = _np.ascontiguousarray(inputs[name])
        arrays[f"in_{name}_dram"] = a
        args.append(nc.dram_tensor(f"in_{name}_dram", a.shape, _mybir.dt.from_np(a.dtype), kind="ExternalInput").ap())
    for i, (shape, dtype) in enumerate(_OUTS):
        dt = _mybir.dt.from_np(_np.dtype(dtype))
        args.append(nc.dram_tensor(f"out_{i}_dram", shape, dt, kind="ExternalOutput").ap())
    gnn_layer_kernel(nc, *args)
    r = _run(nc, [arrays], core_ids=[0])
    return r.results[0]["out_0_dram"]
```

```python
import concourse.bass as bass
from concourse import mybir
from contextlib import ExitStack

P = 128


def gnn_layer_kernel(nc, x, src, dst, rbf, w1, b1, w2, b2, out):
    F32, I32, BF16 = mybir.dt.float32, mybir.dt.int32, mybir.dt.bfloat16
    ALU, ACT, AX = mybir.AluOpType, mybir.ActivationFunctionType, mybir.AxisListType
    ds = bass.ds

    N, C = x.shape
    E, R = rbf.shape
    KC = C // P
    NB = -(-N // P)
    NF = N // P
    NR = N - NF * P
    CB = 7
    EPS = 1e-5

    G = 4
    GE = G * P
    GROUPS = -(-E // GE)
    LAST = GROUPS - 1
    OLD = GROUPS * GE - E
    GT = -(-GROUPS // P)
    GL = GROUPS - (GT - 1) * P
    WN = P - R
    assert NR > 0 and NB % CB == 0 and NB % 2 == 1 and GROUPS % 2 == 1 and 0 < OLD < GE
    K = 4
    assert K == G
    W = C + 1
    QB = 22
    Q = -(-P // QB)
    V = W + Q
    NT = (NB + 1) * P
    U = 4
    H = 2
    D = 4
    ZR = 10
    ZL = [0, 4, 4, 2]
    ZB = [NT // P - (NF // U - 1) * n if k < K - 1 else 0 for k, n in enumerate(ZL)]
    ZA = [NT // P - ZB[k] - (NF // U - 1) * ZL[k] for k in range(K)]
    assert min(ZB) >= 0 and min(ZA) >= 0 and not any(ZA[:K - 1])
    CE = 4
    TS = 4
    FAR = 2 * P

    p_dram = nc.dram_tensor("p_rows", (NB * P, C), F32).ap()
    tables = [nc.dram_tensor(f"table{k}", (NT, W), F32).ap() for k in range(K)]
    ends_dram = nc.dram_tensor("ends", (GT * P, 2), F32).ap()
    halves_dram = nc.dram_tensor("src_halves", (GT * P, 2, GE), BF16).ap()

    rbf_groups = rbf[0:LAST * GE, :].rearrange("(g p j) r -> g p j r", p=P, j=G)
    rbf_last = rbf[E - GE:E, :].rearrange("(p j) r -> p j r", p=P)

    ctx = ExitStack()
    with ctx:
        def sb(name, shape, dt=F32):
            return ctx.enter_context(nc.sbuf_tensor(name, shape, dt))

        def ps(name, shape, dt=F32):
            return ctx.enter_context(nc.psum_tensor(name, shape, dt))

        def sem(name):
            return ctx.enter_context(nc.semaphore(name))

        def sems(name, n):
            return [sem(f"{name}{i}") for i in range(n)]

        ident = sb("ident", [P, P])
        ones2 = sb("ones2", [2, P], BF16)
        w1a = sb("w1a", [P, KC, C])
        w2s = sb("w2s", [P, KC, C])
        b1b = sb("b1b", [P, C])
        b2b = sb("b2b", [P, C])
        area = sb("area", [P, max(4 * G * C, TS // 2 * 2 * K * W, ZR * W)])
        zero = area[:, 0:ZR * W]
        bits = sb("bits", [P, Q])
        belowf = sb("belowf", [P, Q])
        below = sb("below", [P, Q], I32)
        spare = sb("spare", [P, 1])
        silu_table = sb("silu_table", [P, 1])
        window_col = sb("window_col", [P, WN])
        spare_row = sb("spare_row", [P, P, G])
        fresh_row = sb("fresh_row", [P, GE])
        stale_row = sb("stale_row", [P, GE])
        xh = sb("xh", [P, NB, C])
        stats = sb("stats", [P, NB, 6])
        mom = sb("mom", [P, 4, NB])
        rstd = sb("rstd", [P, NB])
        nmr = sb("nmr", [P, NB])
        hs = sb("hs", [P, U, C])
        hT = sb("hT", [P, U, KC, P])
        prow = sb("prow", [P, U, C])
        src_rows = sb("src_rows", [P, GT, GE], I32)
        dst_rows = sb("dst_rows", [P, GT, GE], I32)
        src_f = sb("src_f", [P, GT, GE])
        dst_f = sb("dst_f", [P, GT, GE])
        low = dst_f[:, :, :].bitcast(I32)
        halves = sb("halves", [P, GT, 2, GE], BF16)
        least = sb("least", [P, GT])
        most = sb("most", [P, GT])
        ends = sb("ends_sb", [P, GT, 2])
        moved = sb("moved", [P, GT])
        all_ends = sb("all_ends", [P, GT * P, 2])
        base_words = sb("base_words", [1, GT * P], I32)
        widest = sb("widest", [P, 1])
        windowed = sb("windowed", [P, 1])
        general = sb("general", [P, 1], I32)
        src_cols = sb("src_cols", [P, GT * P * G])
        dst_cols = sb("dst_cols", [P, GT * P * G])
        lead_cols = sb("lead_cols", [P, GT * P * G])
        feats = sb("feats", [P, H, G, R + WN])
        lhs = sb("lhs", [P, H, GE])
        rhs = sb("rhs", [P, H, C])
        src_line = sb("src_line", [2, H, GE], BF16)
        act_rows = sb("act_rows", [P, H, G, V])
        same = sb("same", [P, H, G, P])
        sums = sb("sums", [P, D, G, V])
        words = sb("words", [P, G, Q], I32)
        ahead = sb("ahead", [P, G, Q], I32)
        any_ahead = sb("any_ahead", [P, G])
        shifted = sb("shifted", [P, G])
        rows = sb("rows", [P, D, G], I32)
        dst_index = sb("dst_index", [P, D, G], I32)
        gathered_rows = area[:, 0:2 * G * C].rearrange("p (s j c) -> p s j c", s=2, j=G)
        pre = area[:, 2 * G * C:4 * G * C].rearrange("p (s j c) -> p s j c", s=2, j=G)
        sums_area = sums[:, :, :, :].rearrange("p s j v -> p (s j v)")
        tabs = [half[:, i * 2 * K * W:(i + 1) * 2 * K * W].rearrange("p (b k w) -> p b k w", b=2, k=K)
                for half in (area, sums_area) for i in range(TS // 2)]
        assert U * K // 2 * W <= H * G * V
        pair = act_rows[:, :, :, :].rearrange("p s j v -> p (s j v)")[:, 0:U * K // 2 * W].rearrange(
            "p (s i w) -> p s i w", s=U, i=K // 2)
        cnt = sb("cnt", [P, U, 1])
        base = hs

        ps_t = ps("ps_t", [P, G, P])
        ps_b = ps("ps_b", [P, G, P])
        ps_z = ps("ps_z", [P, G, C])
        ps_s = ps("ps_s", [P, G, 512])
        ps_n = [x.rearrange("p a b -> p (a b)")
                for x in (ps_t[:, :, :], ps_b[:, :, :], ps_z[:, 0:2, :], ps_z[:, 2:4, :])]
        assert U == len(ps_n) == G

        consts_in, consts_done, pool_step = sem("consts_in"), sem("consts_done"), sem("pool_step")
        pool_turn, sp_turn, dve_step, dve_misc = sem("pool_turn"), sem("sp_turn"), sem("dve_step"), sem("dve_misc")
        zero_ready, table_zero, pad_ready = sem("zero_ready"), sems("table_zero", K), sem("pad_ready")
        rows_clear, dst_in, src_in, ends_ready, ends_out = (
            sem("rows_clear"), sem("dst_in"), sem("src_in"), sem("ends_ready"), sem("ends_out"))
        spans_in, general_ready, halves_ready, halves_out = (
            sem("spans_in"), sem("general_ready"), sem("halves_ready"), sem("halves_out"))
        line_ready, cols_ps, cols_sb = sem("line_ready"), sem("cols_ps"), sem("cols_sb")
        x_early, x_in, stats_ready = sem("x_early"), sem("x_in"), sem("stats_ready")
        var_ready, std_ready, norm_ready = sem("var_ready"), sem("std_ready"), sem("norm_ready")
        h_ready, h_added, hT_ps, hT_sb = sem("h_ready"), sem("h_added"), sem("hT_ps"), sem("hT_sb")
        p_ps, p_sb, p_out = sem("p_ps"), sem("p_sb"), sems("p_out", U)
        rbf_in, window_in, line_in = sems("rbf_in", D), sems("window_in", D), sems("line_in", D)
        onehot_ready, lhs_ps, lhs_sb = sem("onehot_ready"), sem("lhs_ps"), sem("lhs_sb")
        z_ps, silu_ready, bcast_ps, same_ready = sem("z_ps"), sem("silu_ready"), sem("bcast_ps"), sem("same_ready")
        sums_ps, sums_sb, lead_step, rows_ready = sem("sums_ps"), sem("sums_sb"), sem("lead_step"), sem("rows_ready")
        scattered = sems("scattered", K)
        index_ready, gathered, pre_ready = sem("index_ready"), sems("gathered", D), sem("pre_ready")
        tabs_in, out_done = sems("tabs_in", TS), sems("out_done", U)
        pair_ready, sT_ps, sT_sb, agg_ps = sem("pair_ready"), sem("sT_ps"), sem("sT_sb"), sem("agg_ps")
        cnt_ready, base_ready, out_ready = sem("cnt_ready"), sem("base_ready"), sem("out_ready")

        block = ctx.enter_context(nc.Block())

        def over(eng, turn, n, whole, end):
            for t in range(n):
                turn(t, 0, t)
            with eng.Fori(1, whole // n) as q:
                for s in range(n):
                    turn(q * n + s, q, s)
            for t in range(whole // n * n, end):
                turn(t, t // n, t % n)

        def over_blocks(eng, turn, behind=0):
            over(eng, turn, U, NF, NB + behind)

        def over_ends(eng, turn, behind=0):
            over(eng, lambda t, q, s: turn(t, q * (2 * TS // U) + s // U, s % U, (q, s // 2)), 2 * TS, NF,
                 NB + behind)

        def over_turns(eng, turn):
            over(eng, turn, D, LAST - 2, LAST + 2)

        def known(t):
            return isinstance(t, int)

        def stage(do, n, count, t, q, s, d, *more):
            if not known(t) or 0 <= t + d < count:
                do(t + d, q + (s + d) // n, (s + d) % n, *more)

        def block_stage(do, t, q, s, d=0, *more):
            stage(do, U, NB, t, q, s, d, *more)

        def group_stage(do, t, q, s, d, *more):
            stage(do, D, GROUPS, t, q, s, d, *more)

        def before(g, slots=H):
            return not known(g) or g >= slots

        def refills(b):
            return not known(b) or b >= U

        def rows_of(b):
            return NR if known(b) and b == NB - 1 else P

        PER_SLOT = [len(range(s, NB, U)) for s in range(U)]

        def zero_pieces(units):
            return [(u, min(ZR, units - u)) for u in range(0, units, ZR)]

        ZEROS = [len(zero_pieces(ZB[k])) + (NF // U - 1) * (ZL[k] > 0) + len(zero_pieces(ZA[k]))
                 for k in range(K)]

        @block.sync
        def _(sp):
            head = (GT - 1) * P

            def load_ends(to, of, arrived):
                sp.dma_start(to[:, 0:GT - 1, :],
                             of[0:head * GE].rearrange("(t r c) -> r t c", r=P, c=GE)).then_inc(arrived, 16)
                sp.dma_start(to[0:GL - 1, GT - 1, :],
                             of[head * GE:LAST * GE].rearrange("(r c) -> r c", c=GE)).then_inc(arrived, 16)
                sp.dma_start(to[GL - 1:GL, GT - 1, :],
                             of[E - GE:E].rearrange("(a c) -> a c", a=1)).then_inc(arrived, 16)

            def load_x(*chunks):
                for c in chunks:
                    lo, hi = c * CB, min((c + 1) * CB, NF)
                    sp.dma_start(xh[:, lo:hi, :],
                                 x[lo * P:hi * P, :].rearrange("(b p) c -> p b c", p=P)
                                 ).then_inc(x_early if c < CE else x_in, 16)

            sp.wait_ge(rows_clear, 2)
            load_ends(dst_rows, dst, dst_in)
            load_ends(src_rows, src, src_in)
            load_x(0, 1)
            sp.wait_ge(ends_ready, 1)
            sp.dma_start(ends_dram.rearrange("(t r) k -> r t k", r=P), ends[:, :, :]).then_inc(ends_out, 16)
            load_x(*range(2, CE))
            sp.wait_ge(ends_out, 16)
            sp.dma_start(all_ends[:, :, :].rearrange("p g k -> p (g k)"),
                         ends_dram.rearrange("g k -> (g k)").partition_broadcast(P)).then_inc(spans_in, 16)
            load_x(*range(CE, NB // CB))
            sp.wait_ge(pad_ready, 1)
            sp.dma_start(xh[0:NR, NF, :], x[NF * P:N, :]).then_inc(x_in, 16)
            sp.wait_ge(halves_ready, 2)
            sp.dma_start(halves_dram.rearrange("(t r) h c -> r t h c", r=P), halves[:, :, :, :]).then_inc(halves_out, 16)

            def store_p(b, q, s):
                sp.wait_ge(p_sb, b + 1)
                sp.sem_inc(sp_turn)
                sp.dma_start(p_dram[ds(b * P, P), :], prow[:, s, :]).then_inc(p_out[s], 16)

            def load_rbf(g, q, s):
                if before(g):
                    sp.wait_ge(lhs_ps, g - H + 1)
                    sp.sem_inc(sp_turn)
                r = rbf_last if known(g) and g == LAST else rbf_groups[ds(g, 1)].rearrange("a p j r -> (a p) j r")
                sp.dma_start(feats[:, s % H, :, 0:R], r).then_inc(rbf_in[s], 16)

            def load_window(g, q, s):
                if before(g):
                    sp.wait_ge(z_ps, g - H + 1)
                    sp.sem_inc(sp_turn)
                first = sp.value_load(base_words[0:1, ds(g, 1)], min_val=0, max_val=NB * P - WN)
                sp.dma_start(rhs[R:P, s % H, :], p_dram[ds(first, WN), :]).then_inc(window_in[s], 16)

            def load_line(g, q, s):
                if before(g):
                    sp.wait_ge(bcast_ps, g - H + 1)
                    sp.sem_inc(sp_turn)
                sp.dma_start(src_line[:, s % H, :], halves_dram[ds(g, 1)].rearrange("a h c -> (a h) c")
                             ).then_inc(line_in[s], 16)

            def stores(t, q, s):
                store_p(t, q, s)
                if known(t) and t == U - 1:
                    sp.wait_ge(halves_out, 16)
                    for g in range(2):
                        load_line(g, 0, g)

            for g in range(2):
                load_rbf(g, 0, g)
            over_blocks(sp, stores)
            for s in range(U):
                sp.wait_ge(p_out[s], 16 * PER_SLOT[s])
            sp.wait_ge(line_ready, 1)

            def loads(t, q, s):
                group_stage(load_window, t, q, s, 0)
                if not known(t) or t > 0:
                    group_stage(load_rbf, t, q, s, 1)
                    group_stage(load_line, t, q, s, 1)
            over_turns(sp, loads)

            for k in range(K):
                sp.wait_ge(scattered[k], 16 * GROUPS)

            def load_tables(b, q, s, pair_slot):
                if s % 2:
                    return
                r, m = pair_slot
                n = 1 if known(b) and b == NB - 1 else 2
                if not known(b) or b >= 2 * TS:
                    sp.wait_ge(pair_ready, b - 2 * TS + 2)
                    sp.sem_inc(sp_turn)
                for k in range(K):
                    sp.dma_start(tabs[m][:, 0:n, k, :],
                                 tables[k][ds(b * P, n * P), :].rearrange("(b p) w -> p b w", p=P)
                                 ).then_inc(tabs_in[m], 16)
            over_ends(sp, load_tables)

        @block.gpsimd
        def _(pool):
            steps = [0]

            def step(ins):
                steps[0] += 1
                ins.then_inc(pool_step, 1)
                pool.wait_ge(pool_step, steps[0])

            step(pool.memset(ident[:, :], 0.0))
            step(pool.affine_select(out=ident[:, :], in_=ident[:, :], compare_op=ALU.not_equal, fill=1.0,
                                    base=0, pattern=[[-1, P]], channel_multiplier=1))
            pool.memset(ones2[:, :], 1.0)
            pool.iota(window_col[:, :], pattern=[[1, WN]], base=0, channel_multiplier=0,
                      allow_small_or_imprecise_dtypes=True)
            pool.iota(spare_row[:, :, :], pattern=[[1, P], [0, G]], base=N, channel_multiplier=0,
                      allow_small_or_imprecise_dtypes=True)
            step(pool.memset(stale_row[:, :], 0.0))
            step(pool.affine_select(out=stale_row[:, :], in_=stale_row[:, :], compare_op=ALU.not_equal,
                                    fill=1.0, base=-(GL - 1), pattern=[[0, GE]], channel_multiplier=1))
            step(pool.affine_select(out=stale_row[:, :], in_=stale_row[:, :], compare_op=ALU.is_gt,
                                    fill=0.0, base=OLD, pattern=[[-1, GE]], channel_multiplier=0))
            step(pool.tensor_scalar(fresh_row[:, :], stale_row[:, :], -1.0, 1.0, ALU.mult, ALU.add))
            step(pool.tensor_tensor(stale_row[:, :], stale_row[:, :],
                                    spare_row[:, :, :].rearrange("p a b -> p (a b)"), ALU.mult))
            pool.iota(spare[:, :], pattern=[[0, 1]], base=N, channel_multiplier=1,
                      allow_small_or_imprecise_dtypes=True).then_inc(consts_done, 1)
            step(pool.memset(bits[:, :], 0.0))
            for i in range(QB):
                step(pool.affine_select(out=bits[:, :], in_=bits[:, :], compare_op=ALU.not_equal,
                                        fill=float(1 << i), base=-i, pattern=[[-QB, Q]], channel_multiplier=1))
            step(pool.memset(belowf[:, :], 0.0))
            for i in range(1, QB):
                step(pool.affine_select(out=belowf[:, :], in_=belowf[:, :], compare_op=ALU.not_equal,
                                        fill=float((1 << i) - 1), base=-i, pattern=[[-QB, Q]],
                                        channel_multiplier=1))
            step(pool.affine_select(out=belowf[:, :], in_=belowf[:, :], compare_op=ALU.is_gt,
                                    fill=float((1 << QB) - 1), base=QB, pattern=[[QB, Q]],
                                    channel_multiplier=-1))
            step(pool.tensor_copy(below[:, :], belowf[:, :]))
            for s in range(H):
                pool.memset(act_rows[:, s, :, C:C + 1], 1.0)
                for j in range(G):
                    last = pool.tensor_copy(act_rows[:, s, j, W:V], bits[:, :])
            last.then_inc(consts_done, 1)

            def add_h(b, q, s):
                pool.wait_ge(h_ready, b + 1)
                pool.tensor_tensor(xh[:, ds(b, 1), :].rearrange("p a c -> p (a c)"),
                                   xh[:, ds(b, 1), :].rearrange("p a c -> p (a c)"), hs[:, s, :],
                                   ALU.add).then_inc(h_added, 1)
            over_blocks(pool, add_h)

            def scatter(g, q, s):
                pool.wait_ge(rows_ready, g + 1)
                pool.sem_inc(pool_turn)
                for j in range(G):
                    if known(g) and g == 0:
                        pool.wait_ge(table_zero[j], 16 * ZEROS[j])
                        pool.sem_inc(pool_turn)
                    if not (known(g) and g == 0):
                        pool.wait_ge(scattered[j], 16 * g)
                        pool.sem_inc(pool_turn)
                    pool.indirect_dma_start(tables[j][:, :], bass.IndirectOffsetOnAxis(rows[:, s, j:j + 1], 0),
                                            sums[:, s, j, 0:W], None, compute_op=ALU.add
                                            ).then_inc(scattered[j], 16)

            def gather(g, q, s):
                pool.wait_ge(index_ready, g + 1)
                if before(g):
                    pool.sem_inc(pool_turn)
                    pool.wait_ge(pre_ready, g - 1)
                pool.sem_inc(pool_turn)
                for j in range(G):
                    pool.indirect_dma_start(gathered_rows[:, s % H, j, :], None, p_dram[:, :],
                                            bass.IndirectOffsetOnAxis(dst_index[:, s, j:j + 1], 0)
                                            ).then_inc(gathered[s], 16)

            for s in range(U):
                pool.wait_ge(p_out[s], 16 * PER_SLOT[s])
            pool.wait_ge(general_ready, 1)
            flag = pool.value_load(general[0:1, 0:1], min_val=0, max_val=1)
            with pool.If(flag):
                for k in range(K):
                    pool.wait_ge(table_zero[k], 16 * ZEROS[k])
                def with_gather(t, q, s):
                    group_stage(gather, t, q, s, 0)
                    group_stage(scatter, t, q, s, -1)
                over_turns(pool, with_gather)
            with pool.Else():
                def scatter_only(t, q, s):
                    group_stage(scatter, t, q, s, -1)
                over_turns(pool, scatter_only)

            def store(b, q, s):
                pool.wait_ge(out_ready, b + 1)
                n = rows_of(b)
                pool.dma_start(out[ds(b * P, n), :], prow[0:n, s, :]).then_inc(out_done[s], 16)
            over_blocks(pool, store)
            for s in range(U):
                pool.wait_ge(out_done[s], 16 * PER_SLOT[s])

        @block.scalar
        def _(act):
            act.wait_ge(src_in, 16 * 3)
            for a, b in ((w1a[:, :, :], w1[0:C, :].rearrange("(k p) c -> p k c", p=P)),
                         *((rhs[0:R, s, :], w1[C:C + R, :]) for s in range(H)),
                         (w2s[:, :, :], w2.rearrange("(k p) c -> p k c", p=P)),
                         (b1b[:, :], b1.partition_broadcast(P)), (b2b[:, :], b2.partition_broadcast(P))):
                act.dma_start(a, b).then_inc(consts_in, 16)
            def copy_cols(n):
                act.wait_ge(cols_ps, n + 1)
                cols = (src_cols, dst_cols)[n // GT]
                t = n % GT
                act.activation(cols[:, t * P * G:(t + 1) * P * G].rearrange("p (g j) -> p j g", j=G),
                               (ps_t, ps_b)[n % 2][:, :, :], ACT.Copy).then_inc(cols_sb, 1)
            for n in range(GT):
                copy_cols(n)

            act.wait_ge(x_in, 16 * (NB // CB - CE + 1))
            act.wait_ge(zero_ready, 1)

            def clear(k, row, n):
                act.dma_start(tables[k][ds(row, n * P), :].rearrange("(p r) w -> p (r w)", p=P),
                              zero[:, 0:n * W]).then_inc(table_zero[k], 16)
            for k in range(K):
                for first, n in zero_pieces(ZB[k]):
                    clear(k, first * P, n)
            for n in range(GT, 2 * GT):
                copy_cols(n)

            act.wait_ge(var_ready, 1)
            act.activation(rstd[:, :], mom[:, 3, :], ACT.Sqrt).then_inc(std_ready, 1)
            act.wait_ge(norm_ready, 1)

            def make_h(b, q, s):
                if refills(b):
                    act.wait_ge(hT_ps, b - U + 1)
                    act.wait_ge(h_added, b - U + 1)
                bb = ds(b, 1)
                act.activation(hs[:, s, :], xh[:, bb, :].rearrange("p a c -> p (a c)"), ACT.Relu,
                               bias=nmr[:, bb], scale=rstd[:, bb]).then_inc(h_ready, 1)

            def copy_hT(b, q, s):
                act.wait_ge(hT_ps, b + 1)
                if refills(b):
                    act.wait_ge(p_ps, b - U + 1)
                act.activation(hT[:, s, :, :].rearrange("p k n -> p (k n)"), ps_n[s][:, 0:C],
                               ACT.Copy).then_inc(hT_sb, 1)

            def node(t, q, s):
                if not known(t) and ZL[s]:
                    clear(s, q * (ZL[s] * P) + (ZB[s] - ZL[s]) * P, ZL[s])
                block_stage(make_h, t, q, s)
                block_stage(copy_hT, t, q, s, -1)
            over_blocks(act, node, 1)

            def copy_lhs(g, q, s):
                act.wait_ge(lhs_ps, g + 1)
                if before(g):
                    act.wait_ge(z_ps, g - H + 1)
                act.activation(lhs[:, s % H, :], ps_t[:, :, :].rearrange("p a b -> p (a b)"),
                               ACT.Copy).then_inc(lhs_sb, 1)

            def silu(g, q, s, gathers):
                act.wait_ge(pre_ready if gathers else z_ps, g + 1)
                if before(g):
                    act.wait_ge(sums_ps, 2 * (g - H + 1))
                act.activation(act_rows[:, s % H, :, 0:C], pre[:, s % H, :, :] if gathers else ps_z[:, :, :],
                               ACT.Silu).then_inc(silu_ready, 1)

            def clear_rest(i, end):
                for first, n in zero_pieces(ZA[K - 1])[i:end]:
                    clear(K - 1, NT - (ZA[K - 1] - first) * P, n)

            def turns(gathers):
                def turn(t, q, s):
                    if known(t) and t == 0:
                        copy_lhs(0, 0, 0)
                        clear_rest(0, 1)
                    group_stage(copy_lhs, t, q, s, 1)
                    if known(t) and t == 0:
                        act.wait_ge(z_ps, 1)
                        clear_rest(1, None)
                    group_stage(silu, t, q, s, 0, gathers)
                over_turns(act, turn)

            act.wait_ge(consts_done, 2)
            act.activation(silu_table[:, :], spare[:, :], ACT.Silu)
            act.wait_ge(general_ready, 1)
            flag = act.value_load(general[0:1, 0:1], min_val=0, max_val=1)
            with act.If(flag):
                turns(True)
            with act.Else():
                turns(False)

            def copy_sT(b, q, s):
                act.wait_ge(sT_ps, b + 1)
                if refills(b):
                    act.wait_ge(agg_ps, b - U + 1)
                act.activation(hT[:, s, :, :].rearrange("p k n -> p (k n)"), ps_n[s][:, 0:C],
                               ACT.Copy).then_inc(sT_sb, 1)
            over_blocks(act, copy_sT)

        @block.tensor
        def _(pe):
            pe.wait_ge(consts_done, 1)
            for n, (rows_, t) in enumerate([(r, t) for r in (src_f, dst_f) for t in range(GT)]):
                if t == 0:
                    pe.wait_ge(halves_ready if rows_ is src_f else line_ready, 1)
                if n >= 2:
                    pe.wait_ge(cols_sb, n - 1)
                bank = (ps_t, ps_b)[n % 2]
                for j in range(G):
                    last = pe.transpose(bank[:, j, :], rows_[:, t, :].rearrange("r (p j) -> r j p", j=G)[:, j, :],
                                        ident[:, :])
                last.then_inc(cols_ps, 1)

            pe.wait_ge(cols_sb, 2 * GT)
            pe.wait_ge(consts_in, 16 * (4 + H))

            def transpose_h(b, q, s):
                pe.wait_ge(h_ready, b + 1)
                if refills(b):
                    pe.wait_ge(hT_sb, b - U + 1)
                for k in range(KC):
                    last = pe.transpose(ps_n[s][:, k * P:(k + 1) * P], hs[:, s, k * P:(k + 1) * P], ident[:, :])
                last.then_inc(hT_ps, 1)

            def product_h(b, q, s):
                pe.wait_ge(hT_sb, b + 1)
                if refills(b):
                    pe.wait_ge(p_sb, b - U + 1)
                for k in range(KC):
                    last = pe.matmul(ps_s[:, s, 0:C], hT[:, s, k, :], w1a[:, k, :],
                                     start=(k == 0), stop=(k == KC - 1))
                last.then_inc(p_ps, 1)

            def node(t, q, s):
                block_stage(transpose_h, t, q, s)
                block_stage(product_h, t, q, s, -1)
            over_blocks(pe, node, 1)
            pe.wait_ge(p_sb, NB)
            pe.wait_ge(consts_done, 2)

            def transpose(g, q, s):
                pe.wait_ge(rbf_in[s], 16 * (q + 1))
                pe.wait_ge(onehot_ready, g + 1)
                if not (known(g) and g == 0):
                    pe.wait_ge(lhs_sb, g)
                for j in range(G):
                    last = pe.transpose(ps_t[:, j, :], feats[:, s % H, j, :], ident[:, :])
                last.then_inc(lhs_ps, 1)

            def product(g, q, s):
                pe.wait_ge(lhs_sb, g + 1)
                pe.wait_ge(window_in[s], 16 * (q + 1))
                if not (known(g) and g == 0):
                    pe.wait_ge(silu_ready, g)
                for j in range(G):
                    last = pe.matmul(ps_z[:, j, :], lhs[:, s % H, j * P:(j + 1) * P], rhs[:, s % H, :],
                                     start=True, stop=True)
                last.then_inc(z_ps, 1)

            def broadcast(g, q, s):
                pe.wait_ge(line_in[s], 16 * (q + 1))
                if not (known(g) and g == 0):
                    pe.wait_ge(same_ready, g)
                pe.matmul(ps_b[:, :, :].rearrange("p a b -> p (a b)"), ones2[:, :], src_line[:, s % H, :],
                          start=True, stop=True).then_inc(bcast_ps, 1)

            def sum_same(g, q, s):
                pe.wait_ge(silu_ready, g + 1)
                pe.wait_ge(same_ready, g + 1)
                for j in range(G):
                    if j % 2 == 0 and not (known(g) and g == 0):
                        pe.wait_ge(sums_sb, 2 * g + j // 2 - 1)
                    last = pe.matmul(ps_s[:, j, 0:V], same[:, s % H, j, :], act_rows[:, s % H, j, :],
                                     start=True, stop=True)
                    if j % 2 == 1:
                        last.then_inc(sums_ps, 1)

            def turn(t, q, s):
                if known(t) and t == 0:
                    transpose(0, 0, 0)
                group_stage(transpose, t, q, s, 1)
                if known(t) and t == 1:
                    sum_same(0, 0, 0)
                group_stage(product, t, q, s, 0)
                group_stage(broadcast, t, q, s, 0)
                if not (known(t) and t == 1):
                    group_stage(sum_same, t, q, s, -1)
            over_turns(pe, turn)
            pe.wait_ge(sums_sb, 2 * GROUPS)

            def transpose_sums(b, q, s):
                pe.wait_ge(pair_ready, b + 1)
                if refills(b):
                    pe.wait_ge(sT_sb, b - U + 1)
                for k in range(KC):
                    for i in range(K // 2):
                        last = pe.matmul(ps_n[s][:, k * P:(k + 1) * P], pair[:, s, i, k * P:(k + 1) * P],
                                         ident[:, :], start=(i == 0), stop=(i == K // 2 - 1))
                last.then_inc(sT_ps, 1)

            def product_sums(b, q, s):
                pe.wait_ge(sT_sb, b + 1)
                if refills(b):
                    pe.wait_ge(out_ready, b - U + 1)
                for k in range(KC):
                    last = pe.matmul(ps_s[:, s, 0:C], hT[:, s, k, :], w2s[:, k, :],
                                     start=(k == 0), stop=(k == KC - 1))
                last.then_inc(agg_ps, 1)

            def finish(t, q, s):
                block_stage(transpose_sums, t, q, s)
                block_stage(product_sums, t, q, s, -1)
            over_blocks(pe, finish, 1)

        @block.vector
        def _(dve):
            steps = [0]

            def chain(ins):
                steps[0] += 1
                ins.then_inc(dve_step, 1)
                dve.wait_ge(dve_step, steps[0])

            dve.memset(dst_rows[:, GT - 1, :], 0).then_inc(rows_clear, 1)
            dve.memset(src_rows[:, GT - 1, :], 0).then_inc(rows_clear, 1)
            dve.memset(xh[:, NF, :], 0.0).then_inc(pad_ready, 1)
            dve.memset(zero[:, :], 0.0).then_inc(zero_ready, 1)

            dve.wait_ge(dst_in, 16 * 3)
            dve.tensor_reduce(least[:, :], dst_rows[:, :, :], AX.X, ALU.min)
            chain(dve.tensor_reduce(most[:, :], dst_rows[:, :, :], AX.X, ALU.max))
            chain(dve.tensor_scalar(ends[:, :, 0], least[:, :], float(NB * P - WN), None, ALU.min))
            dve.tensor_tensor(ends[:, :, 1], most[:, :], ends[:, :, 0], ALU.subtract).then_inc(ends_ready, 1)

            dve.wait_ge(src_in, 16 * 3)
            chain(dve.tensor_copy(src_f[:, :, :], src_rows[:, :, :]))
            dve.wait_ge(consts_done, 1)
            tail = src_f[:, GT - 1, :]
            chain(dve.tensor_tensor(tail, tail, fresh_row[:, :], ALU.mult))
            chain(dve.tensor_tensor(tail, tail, stale_row[:, :], ALU.add))
            chain(dve.tensor_copy(src_rows[:, GT - 1, :], tail))
            chain(dve.tensor_scalar(low, src_rows[:, :, :], 255, None, ALU.bitwise_and))
            by_tile = "r t (p j) -> r t j p"
            for t in range(GT):
                view = halves[:, t, 1, :].rearrange("r (j p) -> r j p", j=G)
                lo = low[:, t, :].rearrange("r (p j) -> r j p", j=G)
                dve.tensor_copy(view, lo)
                view = halves[:, t, 0, :].rearrange("r (j p) -> r j p", j=G)
                last = dve.tensor_tensor(view, src_f[:, t, :].rearrange("r (p j) -> r j p", j=G), lo, ALU.subtract)
            last.then_inc(halves_ready, 1)
            dve.wait_ge(halves_ready, 1)
            dve.sem_inc(halves_ready)

            def block_stats(lo, hi):
                with dve.Fori(lo, hi) as c:
                    for i in range(CB):
                        b = ds(c * CB + i, 1)
                        last = dve.bn_stats(stats[:, b, :].rearrange("p a c -> p (a c)"),
                                            xh[:, b, :].rearrange("p a c -> p (a c)"))
                    last.then_inc(stats_ready, 1)
            dve.wait_ge(x_early, 16 * CE)
            block_stats(0, CE)

            dve.wait_ge(spans_in, 16)
            dve.tensor_copy(base_words[:, :], all_ends[0:1, :, 0])
            chain(dve.tensor_reduce(widest[:, :], all_ends[:, :, 1], AX.X, ALU.max))
            chain(dve.tensor_scalar(windowed[:, :], widest[:, :], float(WN), None, ALU.is_lt))
            dve.tensor_scalar(general[:, :], windowed[:, :], -1.0, 1.0, ALU.mult, ALU.add).then_inc(general_ready, 1)
            chain(dve.tensor_scalar(moved[:, :], ends[:, :, 0], float(FAR), windowed[:, 0:1], ALU.add, ALU.mult))
            chain(dve.tensor_scalar(moved[:, :], moved[:, :], float(-FAR), None, ALU.add))
            for t in range(GT):
                last = dve.tensor_scalar(dst_f[:, t, :], dst_rows[:, t, :], moved[:, t:t + 1], None, ALU.subtract)
            last.then_inc(line_ready, 1)

            dve.wait_ge(x_in, 16 * (NB // CB - CE + 1))
            block_stats(CE, NB // CB)
            dve.wait_ge(stats_ready, NB // CB)
            me, ve, mo, vo = (stats[:, :, i] for i in (1, 2, 4, 5))
            chain(dve.tensor_tensor(mom[:, 0, :], me, mo, ALU.add))
            chain(dve.tensor_tensor(mom[:, 1, :], me, mo, ALU.subtract))
            chain(dve.tensor_tensor(mom[:, 2, :], ve, vo, ALU.add))
            chain(dve.tensor_tensor(mom[:, 1, :], mom[:, 1, :], mom[:, 1, :], ALU.mult))
            chain(dve.tensor_scalar(mom[:, 2, :], mom[:, 2, :], 1.0 / C, EPS, ALU.mult, ALU.add))
            dve.scalar_tensor_tensor(out=mom[:, 3, :], in0=mom[:, 1, :], scalar=0.25, in1=mom[:, 2, :],
                                     op0=ALU.mult, op1=ALU.add).then_inc(var_ready, 1)
            dve.wait_ge(std_ready, 1)
            chain(dve.reciprocal(rstd[:, :], rstd[:, :]))
            dve.scalar_tensor_tensor(out=nmr[:, :], in0=mom[:, 0, :], scalar=-0.5, in1=rstd[:, :],
                                     op0=ALU.mult, op1=ALU.mult).then_inc(norm_ready, 1)
            dve.wait_ge(cols_sb, 2 * GT)
            chain(dve.tensor_scalar(lead_cols[:, :], src_cols[:, :], spare[:, 0:1], None, ALU.subtract))
            dve.wait_ge(consts_in, 16 * (4 + H))

            def add_b1(b, q, s):
                dve.wait_ge(p_ps, b + 1)
                if refills(b):
                    dve.wait_ge(p_out[s], 16 * q)
                dve.tensor_tensor(prow[:, s, :], ps_s[:, s, 0:C], b1b[:, :], ALU.add).then_inc(p_sb, 1)
            over_blocks(dve, add_b1)

            dve.wait_ge(consts_done, 2)

            def onehot(g, q, s):
                if before(g):
                    dve.wait_ge(lhs_ps, g - H + 1)
                dve.tensor_tensor(feats[:, s % H, :, R:R + WN],
                                  window_col[:, :].unsqueeze(1).to_broadcast([P, G, WN]),
                                  dst_cols[:, ds(g * G, G)].unsqueeze(2).to_broadcast([P, G, WN]),
                                  ALU.is_equal).then_inc(onehot_ready, 1)

            def equal_src(g, q, s):
                dve.wait_ge(bcast_ps, g + 1)
                if before(g):
                    dve.wait_ge(sums_ps, 2 * (g - H + 1))
                dve.tensor_tensor(same[:, s % H, :, :], ps_b[:, :, :],
                                  src_cols[:, ds(g * G, G)].unsqueeze(2).to_broadcast([P, G, P]),
                                  ALU.is_equal).then_inc(same_ready, 1)

            def copy_sums(g, q, s):
                for i in range(2):
                    if before(g, D):
                        dve.wait_ge(scattered[2 * i], 16 * (g - D + 1))
                        dve.wait_ge(scattered[2 * i + 1], 16 * (g - D + 1))
                    dve.wait_ge(sums_ps, 2 * g + i + 1)
                    dve.tensor_copy(sums[:, s, 2 * i:2 * i + 2, :],
                                    ps_s[:, 2 * i:2 * i + 2, 0:V]).then_inc(sums_sb, 1)

            def leading_rows(g, q, s):
                def link(ins, n):
                    ins.then_inc(lead_step, 1)
                    dve.wait_ge(lead_step, 4 * g + n)
                dve.wait_ge(sums_sb, 2 * g + 2)
                link(dve.tensor_copy(words[:, :, :], sums[:, s, :, W:V]), 1)
                link(dve.tensor_tensor(ahead[:, :, :], words[:, :, :],
                                       below[:, :].unsqueeze(1).to_broadcast([P, G, Q]), ALU.bitwise_and), 2)
                link(dve.tensor_reduce(any_ahead[:, :], ahead[:, :, :], AX.X, ALU.max), 3)
                link(dve.scalar_tensor_tensor(out=shifted[:, :], in0=any_ahead[:, :], scalar=0.0,
                                              in1=lead_cols[:, ds(g * G, G)], op0=ALU.is_equal, op1=ALU.mult), 4)
                dve.tensor_scalar(rows[:, s, :], shifted[:, :], spare[:, 0:1], None, ALU.add).then_inc(rows_ready, 1)

            def index(g, q, s):
                dve.tensor_scalar(dst_index[:, s, :], dst_cols[:, ds(g * G, G)], float(-FAR), None,
                                  ALU.add).then_inc(index_ready, 1)

            def add_gathered(g, q, s):
                dve.wait_ge(gathered[s], 16 * G * (q + 1))
                dve.wait_ge(z_ps, g + 1)
                if before(g):
                    dve.wait_ge(silu_ready, g - 1)
                dve.tensor_tensor(pre[:, s % H, :, :], ps_z[:, :, :], gathered_rows[:, s % H, :, :],
                                  ALU.add).then_inc(pre_ready, 1)

            def turns(gathers):
                def turn(t, q, s):
                    if known(t) and t == 0:
                        onehot(0, 0, 0)
                        onehot(1, 0, 1)
                        if gathers:
                            index(0, 0, 0)
                    if gathers:
                        group_stage(index, t, q, s, 1)
                    group_stage(onehot, t, q, s, 2)
                    group_stage(equal_src, t, q, s, 0)
                    group_stage(copy_sums, t, q, s, -1)
                    group_stage(leading_rows, t, q, s, -1)
                    if gathers:
                        group_stage(add_gathered, t, q, s, 0)
                over_turns(dve, turn)

            flag = dve.value_load(general[0:1, 0:1], min_val=0, max_val=1)
            with dve.If(flag):
                turns(True)
            with dve.Else():
                turns(False)
            dve.wait_ge(h_added, NB)

            def add_tables(b, q, s, pair_slot):
                r, m = pair_slot
                dve.wait_ge(tabs_in[m], 16 * K * (r + 1))
                if refills(b):
                    dve.wait_ge(sT_ps, b - U + 1)
                dve.tensor_tensor(pair[:, s, :, :], tabs[m][:, s % 2, 0:K // 2, :], tabs[m][:, s % 2, K // 2:K, :],
                                  ALU.add).then_inc(pair_ready, 1)
                dve.wait_ge(pair_ready, b + 1)
                dve.tensor_tensor(cnt[:, s, :], pair[:, s, 0, C:C + 1], pair[:, s, 1, C:C + 1],
                                  ALU.add).then_inc(cnt_ready, 1)

            def add_b2(b, q, s):
                dve.wait_ge(cnt_ready, b + 1)
                dve.scalar_tensor_tensor(out=base[:, s, :], in0=b2b[:, :], scalar=cnt[:, s, :],
                                         in1=xh[:, ds(b, 1), :].rearrange("p a c -> p (a c)"),
                                         op0=ALU.mult, op1=ALU.add).then_inc(base_ready, 1)

            def add_up(b, q, s):
                dve.wait_ge(base_ready, b + 1)
                dve.wait_ge(agg_ps, b + 1)
                if refills(b):
                    dve.wait_ge(out_done[s], 16 * q)
                dve.tensor_tensor(prow[:, s, :], ps_s[:, s, 0:C], base[:, s, :], ALU.add).then_inc(out_ready, 1)

            def finish(t, q, s, pair_slot):
                block_stage(add_tables, t, q, s, 0, pair_slot)
                block_stage(add_b2, t, q, s, -1)
                block_stage(add_up, t, q, s, -2)
            over_ends(dve, finish, 2)


_INS = ['x', 'src', 'dst', 'edge_attr_64', 'L0_gnn_W1', 'L0_gnn_b1', 'L0_gnn_W2', 'L0_gnn_b2']
_OUTS = [((6250, 256), 'float32')]


def kernel(**inputs):
    import numpy as _np
    import concourse.bacc as _bacc
    from concourse import mybir as _mybir
    from concourse.bass_utils import run_bass_kernel_spmd as _run

    nc = _bacc.Bacc("TRN2", target_bir_lowering=False, num_devices=1)
    arrays, args = {}, []
    for name in _INS:
        a = _np.ascontiguousarray(inputs[name])
        arrays[f"in_{name}_dram"] = a
        args.append(nc.dram_tensor(f"in_{name}_dram", a.shape, _mybir.dt.from_np(a.dtype), kind="ExternalInput").ap())
    for i, (shape, dtype) in enumerate(_OUTS):
        dt = _mybir.dt.from_np(_np.dtype(dtype))
        args.append(nc.dram_tensor(f"out_{i}_dram", shape, dt, kind="ExternalOutput").ap())
    gnn_layer_kernel(nc, *args)
    r = _run(nc, [arrays], core_ids=[0])
    return r.results[0]["out_0_dram"]
```
